# Optimizing a Trainium2 kernel written in Bass

```python
import numpy as np
import jax
import jax.numpy as jnp

def _softmax(x, axis=-1):
    return jax.nn.softmax(x, axis=axis)

def _gelu(x):
    return jax.nn.gelu(x, approximate=True)

def _silu(x):
    return jax.nn.silu(x)

def _sigmoid(x):
    return jax.nn.sigmoid(x)

def _layernorm(x, axis=-1, eps=1e-05):
    m = jnp.mean(x, axis=axis, keepdims=True)
    v = jnp.var(x, axis=axis, keepdims=True)
    return (x - m) / jnp.sqrt(v + eps)

def _scatter_add(tgt, idx, src, axis=0):
    return tgt.at[idx].add(src)

def _segment_sum(src, seg, n):
    return jax.ops.segment_sum(src, seg, n)
kernel_name = 'mk_adj_resnorm_d4_adj_r2_d05767'

def setup_inputs(seed: int=0):
    np.random.seed(seed)
    _w = jnp.asarray

    def _rec_inputs():
        import jax
        import jax.numpy as jnp
        _gk = jax.random.key(seed)
        x = -0.000929 + 1 * jax.random.normal(jax.random.fold_in(_gk, 1), (4096, 128), jnp.float32)
        _a = jax.random.bernoulli(jax.random.fold_in(_gk, 2), 0.00390625, (4096, 4096))
        _a = jnp.logical_or(_a, jnp.eye(4096, dtype=bool))
        _af = _a.astype(jnp.float32)
        _af = _af * jax.random.uniform(jax.random.fold_in(_gk, 3), (4096, 4096), jnp.float32, 0.05, 1)
        adj = _af
        return (x, adj)
    x, adj = _rec_inputs()

    def _L0_gnn_setup():
        import jax, jax.numpy as jnp
        import numpy as np
        N = 4096
        F_IN = 128
        F_OUT = 128
        key = jax.random.key(seed)
        k1, k2, k3, k4, k5 = jax.random.split(key, 5)
        x = jax.random.normal(k1, (N, F_IN), dtype=jnp.float32)
        adj = jax.random.uniform(k2, (N, N), dtype=jnp.float32)
        kernel = jax.random.normal(k3, (F_IN, F_OUT), dtype=jnp.float32) * 0.05
        bias = jax.random.normal(k4, (F_OUT,), dtype=jnp.float32) * 0.05
        beta = jax.random.uniform(k5, (N,), dtype=jnp.float32)
        return {'x': x, 'adj': adj, 'kernel': kernel, 'bias': bias, 'beta': beta}
    _L0_gnn_all = _L0_gnn_setup()
    _L0_gnn_in = {k: v for k, v in _L0_gnn_all.items() if k in ('kernel', 'bias', 'beta')}
    del _L0_gnn_all

    def _L1_gnn_setup():
        import jax, jax.numpy as jnp
        import numpy as np
        IN_DIM = 128
        OUT_DIM = 128
        N = 8192
        key = jax.random.key(seed)
        k_x, k_adj, k_w, k_b = jax.random.split(key, 4)
        x = jax.random.normal(k_x, (N, IN_DIM), dtype=jnp.float32)
        adj = jax.random.uniform(k_adj, (N, N), dtype=jnp.float32)
        bound = 1.0 / np.sqrt(2 * IN_DIM)
        W = jax.random.uniform(k_w, (OUT_DIM, 2 * IN_DIM), dtype=jnp.float32, minval=-bound, maxval=bound)
        b = jax.random.uniform(k_b, (OUT_DIM,), dtype=jnp.float32, minval=-bound, maxval=bound)
        return {'x': x, 'adj': adj, 'W': W, 'b': b}
    _L1_gnn_all = _L1_gnn_setup()
    _L1_gnn_in = {k: v for k, v in _L1_gnn_all.items() if k in ('W', 'b')}
    del _L1_gnn_all

    def _L2_gnn_setup():
        import jax, jax.numpy as jnp
        import numpy as np
        N = 8192
        D_IN = 128
        D_OUT = 128
        EPS = 1e-05
        NEG_SLOPE = 0.2
        key = jax.random.key(seed)
        k1, k2, k3, k4 = jax.random.split(key, 4)
        x = jax.random.normal(k1, (N, D_IN), dtype=jnp.float32)
        A = jax.random.uniform(k2, (N, N), dtype=jnp.float32)
        W = jax.random.normal(k3, (D_IN, D_OUT), dtype=jnp.float32) / np.sqrt(D_IN)
        b = jnp.zeros((D_OUT,), dtype=jnp.float32)
        gamma = jnp.ones((D_OUT,), dtype=jnp.float32)
        beta = jnp.zeros((D_OUT,), dtype=jnp.float32)
        del k4
        return {'x': x, 'A': A, 'W': W, 'b': b, 'gamma': gamma, 'beta': beta}
    _L2_gnn_all = _L2_gnn_setup()
    _L2_gnn_in = {k: v for k, v in _L2_gnn_all.items() if k in ('W', 'b', 'gamma', 'beta')}
    del _L2_gnn_all

    def _L3_gnn_setup():
        import jax, jax.numpy as jnp
        import numpy as np
        key = jax.random.key(seed)
        k1, k2, k3, k4 = jax.random.split(key, 4)
        n, in_dim, out_dim = (8192, 128, 128)
        h = jax.random.normal(k1, (n, in_dim), dtype=jnp.float32)
        adj = jax.random.uniform(k2, (n, n), dtype=jnp.float32)
        W_self = jax.random.normal(k3, (in_dim, out_dim), dtype=jnp.float32) * (1.0 / np.sqrt(in_dim))
        W_neigh = jax.random.normal(k4, (in_dim, out_dim), dtype=jnp.float32) * (1.0 / np.sqrt(in_dim))
        return {'h': h, 'adj': adj, 'W_self': W_self, 'W_neigh': W_neigh}
    _L3_gnn_all = _L3_gnn_setup()
    _L3_gnn_in = {k: v for k, v in _L3_gnn_all.items() if k in ('W_self', 'W_neigh')}
    del _L3_gnn_all
    return {'x': x, 'adj': adj, 'L0_gnn_kernel': _L0_gnn_in['kernel'], 'L0_gnn_bias': _L0_gnn_in['bias'], 'L0_gnn_beta': _L0_gnn_in['beta'], 'L1_gnn_W': _L1_gnn_in['W'], 'L1_gnn_b': _L1_gnn_in['b'], 'L2_gnn_W': _L2_gnn_in['W'], 'L2_gnn_b': _L2_gnn_in['b'], 'L2_gnn_gamma': _L2_gnn_in['gamma'], 'L2_gnn_beta': _L2_gnn_in['beta'], 'L3_gnn_W_self': _L3_gnn_in['W_self'], 'L3_gnn_W_neigh': _L3_gnn_in['W_neigh']}

def reference(x, adj, L0_gnn_kernel, L0_gnn_bias, L0_gnn_beta, L1_gnn_W, L1_gnn_b, L2_gnn_W, L2_gnn_b, L2_gnn_gamma, L2_gnn_beta, L3_gnn_W_self, L3_gnn_W_neigh):
    import jax
    import jax.numpy as jnp

    def _L0_gnn_ref(x, adj, kernel, bias, beta):
        import jax, jax.numpy as jnp
        import numpy as np
        N = 4096
        F_IN = 128
        F_OUT = 128
        inv_deg = 1.0 / (jnp.sum(adj, axis=1) + beta)
        agg = adj @ x + beta[:, None] * x
        out = inv_deg[:, None] * agg @ kernel + bias
        return out

    def _L1_gnn_ref(x, adj, W, b):
        import jax, jax.numpy as jnp
        import numpy as np
        IN_DIM = 128
        OUT_DIM = 128
        N = 8192
        h_N = jnp.matmul(adj, x)
        h_cat = jnp.concatenate([x, h_N], axis=-1)
        out = jnp.maximum(jnp.einsum('nd,od->no', h_cat, W) + b, 0.0)
        return out

    def _L2_gnn_ref(x, A, W, b, gamma, beta):
        import jax, jax.numpy as jnp
        import numpy as np
        N = 8192
        D_IN = 128
        D_OUT = 128
        EPS = 1e-05
        NEG_SLOPE = 0.2
        h = A @ (x @ W) + b
        mean = jnp.mean(h, axis=0)
        var = jnp.mean((h - mean) ** 2, axis=0)
        h = gamma * (h - mean) * jax.lax.rsqrt(var + EPS) + beta
        return jnp.where(h >= 0, h, NEG_SLOPE * h)

    def _L3_gnn_ref(h, adj, W_self, W_neigh):
        import jax, jax.numpy as jnp
        import numpy as np
        deg = jnp.clip(jnp.sum(adj, axis=1, keepdims=True), 1.0)
        h_neigh = adj @ h / deg
        return h @ W_self + h_neigh @ W_neigh
    x = _layernorm(x + _L0_gnn_ref(x, adj, L0_gnn_kernel, L0_gnn_bias, L0_gnn_beta), axis=-1)
    x = _layernorm(x + _L1_gnn_ref(x, adj, L1_gnn_W, L1_gnn_b), axis=-1)
    x = _layernorm(x + _L2_gnn_ref(x, adj, L2_gnn_W, L2_gnn_b, L2_gnn_gamma, L2_gnn_beta), axis=-1)
    x = _layernorm(x + _L3_gnn_ref(x, adj, L3_gnn_W_self, L3_gnn_W_neigh), axis=-1)
    return x

_drawn_inputs = setup_inputs


def setup_inputs(seed=0):
    import zlib

    import numpy as np

    out = dict(_drawn_inputs(seed))
    spreads = {'L2_gnn_b': (0.0, 0.8), 'L2_gnn_gamma': (1.0, 0.2), 'L2_gnn_beta': (0.0, 0.1)}
    factors = {'L0_gnn_beta': 2.918}
    for name, (base, spread) in spreads.items():
        noise = np.random.default_rng([zlib.crc32(name.encode()), seed]).standard_normal(out[name].shape)
        drawn = base * np.exp(spread * noise) if base else spread * noise
        out[name] = jnp.asarray(drawn.astype(out[name].dtype))
    for name, factor in factors.items():
        out[name] = (out[name] * factor).astype(out[name].dtype)
    return out
```

```python
from contextlib import ExitStack

import concourse.bass as bass
from concourse import mybir

NODES, FEATURES, LAYERS = 4096, 128, 4
P = 128
QUADRANTS, QUAD = 4, 32
CHUNK = 512
CHUNKS = NODES // CHUNK
TILE_COLUMNS = 1024
TILES = NODES // TILE_COLUMNS
QUAD_COLUMNS = TILE_COLUMNS // QUADRANTS
GROUPS = CHUNK // QUAD
BLOCKS = NODES // P
PAIRS = BLOCKS // 2
TILE_PAIRS = PAIRS // TILES
TILE_BLOCKS = BLOCKS // TILES
ROW_BLOCKS = CHUNK // P
RING = 4
PART_RING = 2
SPLIT = [1, 2, 4, 5, 7, 8, 10, 11, 13, 14]
SPLITS = len(SPLIT)
DEGREE, CONCAT, BATCHNORM, SAGE = range(4)
EPS = 1e-5
SLOPE = 0.2
LOAD = 16 * QUADRANTS
MOVE = 16 * 8


def is_number(value):
    return isinstance(value, int)


def gnn_layers(nc, x, adj, w_degree, bias_degree, self_loop, w_concat, bias_concat, w_batch, bias_batch,
               gamma, shift_batch, w_self, w_neighbour, out):
    f32, f32r = mybir.dt.float32, mybir.dt.float32r
    ACT, ALU, AXIS = mybir.ActivationFunctionType, mybir.AluOpType, mybir.AxisListType
    ds = bass.ds

    adj_tiles = adj.rearrange("(c g r) (t q f) -> c t q r g f", g=GROUPS, r=QUAD, q=QUADRANTS, t=TILES)
    x_by_block = x.rearrange("(t q b j) d -> t q j b d", t=TILES, q=QUADRANTS, j=QUAD)
    x_by_chunk = x.rearrange("(b p) d -> p b d", p=P)
    out_by_chunk = out.rearrange("(c b p) d -> c p b d", p=P, b=ROW_BLOCKS)

    with ExitStack() as ctx:
        def sbuf(name, shape, dtype=f32):
            return ctx.enter_context(nc.sbuf_tensor(name, shape, dtype))

        def psum(name, shape):
            return ctx.enter_context(nc.psum_tensor(name, shape, f32))

        def sem(name):
            return ctx.enter_context(nc.semaphore(name))

        raw = sbuf("raw", [P, TILES, GROUPS, QUAD_COLUMNS])
        turned = sbuf("turned", [P, RING, 2, CHUNK])
        high = sbuf("high", [P, PART_RING, 2, CHUNK], f32r)
        low = sbuf("low", [P, PART_RING, 2, CHUNK], f32r)
        x_rows = sbuf("x_rows", [P, BLOCKS, FEATURES])
        x_moved = sbuf("x_moved", [P, BLOCKS, FEATURES])
        x_blocks = sbuf("x_blocks", [P, BLOCKS, FEATURES])
        x_high = sbuf("x_high", [P, SPLITS, 2, FEATURES], f32r)
        x_low = sbuf("x_low", [P, SPLITS, 2, FEATURES], f32r)
        x_chunk = sbuf("x_chunk", [P, ROW_BLOCKS, FEATURES])
        x_chunk_t = sbuf("x_chunk_t", [P, CHUNK])
        agg_t = sbuf("agg_t", [P, CHUNK])
        h_t = sbuf("h_t", [P, CHUNKS, CHUNK])
        half = h_t[:, 0:4, :].rearrange("p a (b c) -> p (a b) c", b=4)
        quarter = h_t[:, 4:6, :].rearrange("p a (b c) -> p (a b) c", b=8)
        loops = h_t[:, 6, :].rearrange("p (b c) -> p b c", b=ROW_BLOCKS)
        leaky = sbuf("leaky", [P, 2, CHUNK])
        new = sbuf("new", [P, 2, ROW_BLOCKS, FEATURES])
        stats = sbuf("stats", [P, 2, ROW_BLOCKS, 6])
        mean_var = sbuf("mean_var", [P, 2, ROW_BLOCKS, 2])
        var_eps = sbuf("var_eps", [P, 2, ROW_BLOCKS])
        std = sbuf("std", [P, 2, ROW_BLOCKS])
        rstd = sbuf("rstd", [P, 2, ROW_BLOCKS])
        newton = sbuf("newton", [P, 2, ROW_BLOCKS])
        row_parts = sbuf("row_parts", [P, GROUPS, TILES])
        row_sums = sbuf("row_sums", [P, GROUPS])
        degree = sbuf("degree", [P, ROW_BLOCKS])
        inv_looped = sbuf("inv_looped", [P, ROW_BLOCKS])
        inv_degree = sbuf("inv_degree", [P, BLOCKS])
        bn_stats = sbuf("bn_stats", [P, CHUNKS, 6])
        bn_mean_var = sbuf("bn_mean_var", [P, 2])
        bn_var_eps = sbuf("bn_var_eps", [P, 1])
        bn_std = sbuf("bn_std", [P, 1])
        bn_rstd = sbuf("bn_rstd", [P, 1])
        bn_newton = sbuf("bn_newton", [P, 1])
        bn_scale = sbuf("bn_scale", [P, 1])
        bn_shift = sbuf("bn_shift", [P, 1])
        ident = sbuf("ident", [P, P])
        fold = sbuf("fold", [P, 3 * QUAD + P])
        loop_rows = sbuf("loop_rows", [P, BLOCKS])
        w0 = sbuf("w0", [P, FEATURES])
        w1 = sbuf("w1", [P, 2 * FEATURES])
        w1_t = sbuf("w1_t", [P, 2, FEATURES])
        w2 = sbuf("w2", [P, FEATURES])
        w3_self = sbuf("w3_self", [P, FEATURES])
        w3_neighbour = sbuf("w3_neighbour", [P, FEATURES])
        bias0 = sbuf("bias0", [P, 1, FEATURES])
        bias1 = sbuf("bias1", [P, 1, FEATURES])
        bias2 = sbuf("bias2", [P, 1])
        gamma2 = sbuf("gamma2", [P, 1])
        beta2 = sbuf("beta2", [P, 1])
        agg = psum("agg", [P, 2, CHUNK])
        y = psum("y", [P, CHUNK])
        y_self = psum("y_self", [P, CHUNK])
        x_turned = psum("x_turned", [P, CHUNK])
        sums = psum("sums", [P, CHUNK])
        h_turned = psum("h_turned", [P, 2, CHUNK])
        y_rows = y[:, :].rearrange("p (b d) -> p b d", b=ROW_BLOCKS)
        y_self_rows = y_self[:, :].rearrange("p (b d) -> p b d", b=ROW_BLOCKS)

        tile_loaded = [sem(f"tile_loaded_{t}") for t in range(TILES)]
        blocks_loaded = [sem(f"blocks_loaded_{t}") for t in range(TILES)]
        rows_loaded, constants_loaded = sem("rows_loaded"), sem("constants_loaded")
        bits_made, identity_made = sem("bits_made"), sem("identity_made")
        w1_turned, w1_copied = sem("w1_turned"), sem("w1_copied")
        pair_turned, pair_used = sem("pair_turned"), sem("pair_used")
        high_ready, low_ready = sem("high_ready"), sem("low_ready")
        agg_copied, y_done, y_read = sem("agg_copied"), sem("y_done"), sem("y_read")
        chunk_staged, loops_made, loops_added = sem("chunk_staged"), sem("loops_made"), sem("loops_added")
        chunk_turned, chunk_t_copied = sem("chunk_turned"), sem("chunk_t_copied")
        half_folded, quarter_folded = sem("half_folded"), sem("quarter_folded")
        tile_summed, rows_summed, degree_done = sem("tile_summed"), sem("rows_summed"), sem("degree_done")
        var_ready, std_ready, x_normed = sem("var_ready"), sem("std_ready"), sem("x_normed")
        moved = [sem("moved_even"), sem("moved_odd")]
        operand_high, operand_low = sem("operand_high"), sem("operand_low")
        bn_counted = sem("bn_counted")
        bn_var_ready, bn_std_ready, bn_ready = sem("bn_var_ready"), sem("bn_std_ready"), sem("bn_ready")
        affine_done, leaky_done, h_back = sem("affine_done"), sem("leaky_done"), sem("h_back")
        vector_step, stored = sem("vector_step"), sem("stored")
        block = ctx.enter_context(nc.Block())

        @block.sync
        def _(sp):
            def load(layer, c, t):
                k = CHUNKS * layer + c
                if not (is_number(k) and k == 0):
                    if layer == DEGREE or is_number(c) and c == 0 and layer == CONCAT:
                        sp.wait_ge(quarter_folded, TILES * (k - 1) + t + 1)
                    else:
                        sp.wait_ge(pair_turned, PAIRS * (k - 1) + TILE_PAIRS * (t + 1))
                for q in (0, 2, 1, 3):
                    lanes = slice(QUAD * q, QUAD * (q + 1))
                    if is_number(c):
                        source = adj_tiles[c, t, q]
                    else:
                        source = adj_tiles[ds(c, 1), t, q].rearrange("a r g f -> (a r) g f")
                    sp.dma_start(raw[lanes, t, :, :], source).then_inc(tile_loaded[t], 16)

            def move(layer, c, t, odd):
                sp.wait_ge(x_normed, CHUNKS * layer + c + 1)
                if layer > 0:
                    sp.wait_ge(operand_high, PAIRS * layer)
                    sp.wait_ge(operand_low, SPLITS * layer)
                if not (is_number(t) and t == 0 and layer == 0):
                    sp.wait_ge(moved[odd], MOVE * (TILES * layer + t))
                for a in range(2):
                    for u in range(4):
                        q = 2 * odd + a
                        sp.dma_start(
                            x_moved[QUAD * q:QUAD * (q + 1), ds(TILE_BLOCKS * t + u, 2, step=4), :],
                            x_rows[QUAD * u:QUAD * (u + 1), ds(ROW_BLOCKS * c + 2 * a, 2), :],
                        ).then_inc(moved[odd], 16)

            def store(c):
                sp.wait_ge(x_normed, CHUNKS * SAGE + c + 1)
                if is_number(c):
                    target = out_by_chunk[c]
                else:
                    target = out_by_chunk[ds(c, 1)].rearrange("a p b d -> (a p) b d")
                sp.dma_start(target, x_rows[:, ds(ROW_BLOCKS * c, ROW_BLOCKS), :]).then_inc(stored, 16)

            for layer in range(LAYERS):
                load(layer, 0, 0)
                if layer > 0 and layer - 1 != BATCHNORM:
                    move(layer - 1, CHUNKS - 2, TILES - 1, 0)
                for t in range(1, TILES):
                    load(layer, 0, t)
                load(layer, 1, 0)
                if layer > 0:
                    if layer - 1 != BATCHNORM:
                        move(layer - 1, CHUNKS - 1, TILES - 1, 1)
                        for t in range(1, TILES):
                            load(layer, 1, t)
                    else:
                        for t in range(TILES):
                            move(BATCHNORM, 2 * t, t, 0)
                            move(BATCHNORM, 2 * t + 1, t, 1)
                            if t > 0:
                                load(layer, 1, t)
                else:
                    for t in range(1, TILES):
                        load(layer, 1, t)

                def two_chunks(t2):
                    for odd in range(2):
                        c = 2 * t2 + odd
                        load(layer, c, 0)
                        if layer == SAGE:
                            store(c - 2)
                        elif layer != BATCHNORM:
                            move(layer, c - 2, t2 - 1, odd)
                        for t in range(1, TILES):
                            load(layer, c, t)

                if layer == 0:
                    two_chunks(1)
                with sp.Fori(2 if layer == 0 else 1, CHUNKS // 2) as t2:
                    two_chunks(t2)
            store(CHUNKS - 2)
            store(CHUNKS - 1)
            sp.wait_ge(stored, 16 * CHUNKS)

        @block.gpsimd
        def _(pool):
            nc.gpsimd.memset(ident[:, :], 0.0).then_inc(bits_made, 1)
            nc.gpsimd.memset(fold[:, :], 0.0).then_inc(bits_made, 1)
            pool.wait_ge(bits_made, 2)
            nc.gpsimd.affine_select(out=ident[:, :], in_=ident[:, :], compare_op=ALU.not_equal, fill=1.0,
                                    base=0, pattern=[[-1, P]], channel_multiplier=1).then_inc(identity_made, 1)
            pool.wait_ge(identity_made, 1)
            middle = fold[:, 3 * QUAD:4 * QUAD]
            for q in range(QUADRANTS):
                nc.gpsimd.tensor_tensor(middle, middle, ident[:, QUAD * q:QUAD * (q + 1)],
                                        ALU.add).then_inc(identity_made, 1)
                pool.wait_ge(identity_made, q + 2)

            def fold_tile(c, t):
                n = TILES * c + t
                pool.wait_ge(tile_loaded[t], LOAD * (c + 1))
                nc.gpsimd.tensor_tensor(half, raw[:, t, :, 0:QUAD_COLUMNS // 2],
                                        raw[:, t, :, QUAD_COLUMNS // 2:QUAD_COLUMNS],
                                        ALU.add).then_inc(half_folded, 1)
                pool.wait_ge(half_folded, n + 1)
                if not (is_number(n) and n == 0):
                    pool.wait_ge(tile_summed, n)
                pool.wait_ge(pair_turned, PAIRS * c + TILE_PAIRS * (t + 1))
                nc.gpsimd.tensor_tensor(quarter, half[:, :, 0:64], half[:, :, 64:128],
                                        ALU.add).then_inc(quarter_folded, 1)
                pool.wait_ge(quarter_folded, n + 1)

            def low_part(layer, c, n):
                s = SPLIT.index(n)
                pool.wait_ge(high_ready, SPLITS * (CHUNKS * (layer - 1) + c) + s + 1)
                nc.gpsimd.tensor_tensor(low[:, s % PART_RING], turned[:, n % RING],
                                        high[:, s % PART_RING].bitcast(f32),
                                        ALU.subtract).then_inc(low_ready, 1)

            def low_operand(layer, n):
                s = SPLIT.index(n)
                pool.wait_ge(operand_high, PAIRS * (layer - 1) + n + 1)
                nc.gpsimd.tensor_tensor(x_low[:, s], x_moved[:, 2 * n:2 * n + 2, :], x_high[:, s].bitcast(f32),
                                        ALU.subtract).then_inc(operand_low, 1)

            def operands_of_tile(layer, t):
                for n in SPLIT:
                    if n // TILE_PAIRS == t:
                        low_operand(layer, n)

            for t in range(TILES):
                fold_tile(0, t)
            with pool.Fori(1, CHUNKS - 1) as c:
                for t in range(TILES):
                    fold_tile(c, t)
            for t in range(TILES):
                fold_tile(CHUNKS - 1, t)
            for t in range(TILES - 1):
                operands_of_tile(1, t)
            for layer in range(1, LAYERS):
                after_batchnorm = layer - 1 == BATCHNORM
                for n in SPLIT:
                    if after_batchnorm and n in (1, 4, 8, 13):
                        operands_of_tile(layer, n // TILE_PAIRS)
                    low_part(layer, 0, n)
                    if n == 8 and not after_batchnorm:
                        operands_of_tile(layer, TILES - 1)
                with pool.Fori(1, CHUNKS - 1) as c:
                    for n in SPLIT:
                        low_part(layer, c, n)
                for n in SPLIT:
                    low_part(layer, CHUNKS - 1, n)
                    if layer < BATCHNORM and n in (8, 13):
                        operands_of_tile(layer + 1, 0 if n == 8 else 1)
                if layer < BATCHNORM:
                    operands_of_tile(layer + 1, 2)

        @block.scalar
        def _(act):
            for t in range(TILES):
                for q in range(QUADRANTS):
                    act.dma_start(x_blocks[QUAD * q:QUAD * (q + 1), TILE_BLOCKS * t:TILE_BLOCKS * (t + 1), :],
                                  x_by_block[t, q]).then_inc(blocks_loaded[t], 16)
            act.dma_start(x_rows[:, :, :], x_by_chunk).then_inc(rows_loaded, 16)
            column = [(bias2, bias_batch), (gamma2, gamma), (beta2, shift_batch)]
            loads = [(w0[:, :], w_degree), (w1[:, :], w_concat), (w2[:, :], w_batch), (w3_self[:, :], w_self),
                     (w3_neighbour[:, :], w_neighbour),
                     (bias0[:, 0, :], bias_degree.partition_broadcast(P)),
                     (bias1[:, 0, :], bias_concat.partition_broadcast(P))]
            loads += [(to[:, :], a.rearrange("(p a) -> p a", a=1)) for to, a in column]
            for to, a in loads:
                act.dma_start(to, a).then_inc(constants_loaded, 16)
            with nc.allow_non_contiguous_dma(reason="4096 numbers, once"):
                act.dma_start(loop_rows[:, :], self_loop.rearrange("(b p) -> p b", p=P)).then_inc(constants_loaded, 16)
            act.wait_ge(w1_turned, 1)
            nc.scalar.activation(w1_t[:, :, :], x_turned[:, 0:2 * FEATURES].rearrange("p (a b) -> p a b", a=2),
                                 ACT.Copy).then_inc(w1_copied, 1)

            def high_part(layer, c, n):
                s = SPLIT.index(n)
                k = CHUNKS * layer + c
                act.wait_ge(pair_turned, PAIRS * k + n + 1)
                if s >= PART_RING:
                    act.wait_ge(pair_used, PAIRS * k + SPLIT[s - PART_RING] + 1)
                elif not (is_number(k) and k == CHUNKS):
                    act.wait_ge(pair_used, PAIRS * (k - 1) + SPLIT[s - PART_RING] + 1)
                nc.scalar.activation(high[:, s % PART_RING], turned[:, n % RING], ACT.Copy).then_inc(high_ready, 1)

            def copy_agg(layer, c, parity):
                e = CHUNKS * layer + c
                act.wait_ge(pair_used, PAIRS * (e + 1))
                if not (is_number(e) and e == 0):
                    act.wait_ge(y_done, e)
                nc.scalar.activation(agg_t[:, :], agg[:, parity, :] if is_number(parity) else
                                     agg[:, ds(parity, 1), :].rearrange("p a n -> p (a n)"),
                                     ACT.Copy).then_inc(agg_copied, 1)

            def stage_chunk(layer, c):
                e = CHUNKS * layer + c
                if layer == DEGREE:
                    if is_number(c) and c == 0:
                        act.wait_ge(rows_loaded, 16)
                        act.wait_ge(constants_loaded, 16 * (len(loads) + 1))
                        act.wait_ge(identity_made, 1)
                    else:
                        act.wait_ge(loops_added, c)
                else:
                    before = 0 if layer == CONCAT else CHUNKS
                    if is_number(c) and c == 0 and layer == CONCAT:
                        act.wait_ge(loops_added, CHUNKS)
                    else:
                        act.wait_ge(chunk_turned, before + c)
                    act.wait_ge(x_normed, e - CHUNKS + 1)
                nc.scalar.activation(x_chunk[:, :, :], x_rows[:, ds(ROW_BLOCKS * c, ROW_BLOCKS), :],
                                     ACT.Copy).then_inc(chunk_staged, 1)
                if layer == DEGREE:
                    for b in range(ROW_BLOCKS):
                        made = nc.scalar.activation(loops[:, b, :], ident[:, :], ACT.Copy,
                                                    scale=loop_rows[:, ds(ROW_BLOCKS * c + b, 1)])
                    made.then_inc(loops_made, 1)

            def copy_chunk_t(layer, c):
                n = (0 if layer == CONCAT else CHUNKS) + c
                act.wait_ge(chunk_turned, n + 1)
                act.wait_ge(y_done, CHUNKS * layer + c)
                nc.scalar.activation(x_chunk_t[:, :], x_turned[:, :], ACT.Copy).then_inc(chunk_t_copied, 1)

            def root(layer, c, parity=0):
                act.wait_ge(var_ready, CHUNKS * layer + c + 1)
                nc.scalar.activation(std[:, parity, :], var_eps[:, parity, :], ACT.Sqrt).then_inc(std_ready, 1)

            def high_operands(layer, t):
                for odd in range(2):
                    act.wait_ge(moved[odd], MOVE * (TILES * (layer - 1) + t + 1))
                act.wait_ge(pair_used, PAIRS * (CHUNKS * layer - 1) + TILE_PAIRS * (t + 1))
                for n in range(TILE_PAIRS * t, TILE_PAIRS * (t + 1)):
                    to = x_high[:, SPLIT.index(n)] if n in SPLIT else x_blocks[:, 2 * n:2 * n + 2, :]
                    nc.scalar.activation(to, x_moved[:, 2 * n:2 * n + 2, :], ACT.Copy).then_inc(operand_high, 1)

            stage_chunk(DEGREE, 0)
            with act.Fori(1, CHUNKS) as c:
                copy_agg(DEGREE, c - 1, (c + 1) % 2)
                stage_chunk(DEGREE, c)
                root(DEGREE, c - 1)
            for t in range(TILES - 1):
                high_operands(CONCAT, t)

            def chunk(layer, c, before):
                first = is_number(c) and c == 0
                last_c = CHUNKS - 1 if first else c - 1
                high_part(layer, c, 1)
                high_part(layer, c, 2)
                copy_agg(before, last_c, 1 if first else (c + 1) % 2)
                if layer in (CONCAT, SAGE):
                    stage_chunk(layer, c)
                high_part(layer, c, 4)
                high_part(layer, c, 5)
                if before != BATCHNORM:
                    root(before, last_c)
                high_part(layer, c, 7)
                high_part(layer, c, 8)
                if first:
                    high_operands(layer, TILES - 1)
                elif is_number(c) and layer < BATCHNORM:
                    high_operands(layer + 1, 0)
                for n in (10, 11, 13):
                    high_part(layer, c, n)
                if is_number(c) and not first and layer < BATCHNORM:
                    high_operands(layer + 1, 1)
                high_part(layer, c, 14)
                if layer in (CONCAT, SAGE):
                    copy_chunk_t(layer, c)
                if is_number(c) and not first and layer < BATCHNORM:
                    high_operands(layer + 1, 2)

            for layer in (CONCAT, BATCHNORM):
                chunk(layer, 0, layer - 1)
                with act.Fori(1, CHUNKS - 1) as c:
                    chunk(layer, c, layer)
                chunk(layer, CHUNKS - 1, layer)

            copy_agg(BATCHNORM, CHUNKS - 1, 1)
            act.wait_ge(bn_var_ready, 1)
            nc.scalar.activation(bn_std[:, :], bn_var_eps[:, :], ACT.Sqrt).then_inc(bn_std_ready, 1)
            act.wait_ge(bn_ready, 1)

            def finish_batchnorm(t):
                for c in (2 * t, 2 * t + 1):
                    nc.scalar.activation(h_t[:, c, :], h_t[:, c, :], ACT.Identity, bias=bn_shift[:, :],
                                         scale=bn_scale[:, :]).then_inc(affine_done, 1)
                for c in (2 * t, 2 * t + 1):
                    root(BATCHNORM, c, c % 2)

            finish_batchnorm(0)
            finish_batchnorm(1)
            for t, pairs in enumerate(((1, 2), (4, 5, 7), (8, 10, 11), (13, 14))):
                high_operands(SAGE, t)
                if t == 0:
                    stage_chunk(SAGE, 0)
                for n in pairs:
                    high_part(SAGE, 0, n)
                if t < 2:
                    finish_batchnorm(t + 2)
            copy_chunk_t(SAGE, 0)
            with act.Fori(1, CHUNKS) as c:
                chunk(SAGE, c, SAGE)
            copy_agg(SAGE, CHUNKS - 1, 1)
            root(SAGE, CHUNKS - 1)

        @block.vector
        def _(dve):
            def turn(layer, c, n):
                k = CHUNKS * layer + c
                t, at = n // TILE_PAIRS, 64 * (n % TILE_PAIRS)
                if n % TILE_PAIRS == 0:
                    dve.wait_ge(tile_loaded[t], LOAD * (k + 1))
                if not (is_number(k) and k == 0 and n < RING):
                    dve.wait_ge(pair_used, PAIRS * k + n - RING + 1)
                nc.vector.transpose(turned[:, n % RING].rearrange("p b (g r) -> p g b r", g=GROUPS),
                                    raw[:, t, :, at:at + 64].rearrange("p g (b j) -> p g b j", b=2),
                                    ).then_inc(pair_turned, 1)

            def sum_tile(c, t):
                n = TILES * c + t
                dve.wait_ge(quarter_folded, n + 1)
                if t == 0 and not is_number(c):
                    dve.wait_ge(rows_summed, c)
                nc.vector.tensor_reduce(row_parts[:, :, t], quarter, AXIS.X, ALU.add).then_inc(tile_summed, 1)

            def sum_rows(c):
                dve.wait_ge(tile_summed, TILES * (c + 1))
                if not is_number(c):
                    dve.wait_ge(degree_done, c)
                nc.vector.tensor_reduce(row_sums[:, :], row_parts[:, :, :], AXIS.X, ALU.add).then_inc(rows_summed, 1)

            norm_steps, refine_steps = 7, 5
            steps_of = [6 + norm_steps, 1 + norm_steps, 1 + norm_steps, 2 + norm_steps]
            first_step = [0]
            for layer in range(SAGE):
                first_step.append(first_step[-1] + CHUNKS * steps_of[layer] + (layer == BATCHNORM) * (refine_steps + 2))

            def stepper(base):
                done = [0]

                def step(instruction):
                    done[0] += 1
                    instruction.then_inc(vector_step, 1)
                    dve.wait_ge(vector_step, base + done[0])
                return step, done

            def statistics(e, step, parity=0):
                for b in range(ROW_BLOCKS):
                    last = nc.vector.bn_stats(stats[:, parity, b, :], new[:, parity, b, :])
                step(last)
                nc.vector.memset(var_eps[:, parity, :], EPS)
                for b in range(ROW_BLOCKS):
                    last = nc.vector.bn_aggr(mean_var[:, parity, b, :], stats[:, parity, b, :])
                step(last)
                nc.vector.tensor_tensor(var_eps[:, parity, :], mean_var[:, parity, :, 1], var_eps[:, parity, :],
                                        ALU.add).then_inc(var_ready, 1)

            def refine(step, r, root_of, square, scratch):
                step(nc.vector.reciprocal(r, root_of))
                step(nc.vector.tensor_tensor(scratch, square, r, ALU.mult))
                step(nc.vector.tensor_tensor(scratch, scratch, r, ALU.mult))
                step(nc.vector.tensor_scalar(scratch, scratch, -0.5, 1.5, ALU.mult, ALU.add))
                step(nc.vector.tensor_tensor(r, r, scratch, ALU.mult))

            def normalize(e, c, step, parity=0):
                dve.wait_ge(std_ready, e + 1)
                refine(step, rstd[:, parity, :], std[:, parity, :], var_eps[:, parity, :], newton[:, parity, :])
                for b in range(ROW_BLOCKS):
                    row = x_rows[:, ds(ROW_BLOCKS * c + b, 1), :].rearrange("p a d -> p (a d)")
                    last = nc.vector.tensor_scalar(row, new[:, parity, b, :], mean_var[:, parity, b, 0:1],
                                                   rstd[:, parity, b:b + 1], ALU.subtract, ALU.mult)
                last.then_inc(x_normed, 1)

            def combine(layer, c):
                e = CHUNKS * layer + c
                step, done = stepper(first_step[layer] + steps_of[layer] * c)
                now = new[:, 0]
                rows = x_rows[:, ds(ROW_BLOCKS * c, ROW_BLOCKS), :]

                def by_row(a):
                    return a.unsqueeze(2).to_broadcast([P, ROW_BLOCKS, FEATURES])

                if layer == DEGREE:
                    blocks = ds(ROW_BLOCKS * c, ROW_BLOCKS)
                    dve.wait_ge(degree_done, c + 1)
                    step(nc.vector.tensor_tensor(degree[:, :], sums[:, 0:ROW_BLOCKS], loop_rows[:, blocks], ALU.add))
                    step(nc.vector.reciprocal(inv_looped[:, :], degree[:, :]))
                    step(nc.vector.tensor_scalar(degree[:, :], sums[:, 0:ROW_BLOCKS], 1.0, None, ALU.max))
                    step(nc.vector.reciprocal(inv_degree[:, blocks], degree[:, :]))
                dve.wait_ge(y_done, e + 1)
                if layer == BATCHNORM:
                    if is_number(c) and c == 0:
                        pass
                    nc.vector.tensor_scalar(h_t[:, c, :] if is_number(c) else
                                            h_t[:, ds(c, 1), :].rearrange("p a n -> p (a n)"),
                                            y[:, :], bias2[:, 0:1], None, ALU.add).then_inc(y_read, 1)
                    dve.wait_ge(y_read, e + 1)
                    nc.vector.bn_stats(bn_stats[:, ds(c, 1), :].rearrange("p a n -> p (a n)"),
                                       h_t[:, ds(c, 1), :].rearrange("p a n -> p (a n)")).then_inc(bn_counted, 1)
                    return None
                if not (is_number(e) and e == 0):
                    dve.wait_ge(x_normed, e)
                if layer == DEGREE:
                    nc.vector.tensor_tensor(now, y_rows, by_row(inv_looped[:, :]), ALU.mult).then_inc(y_read, 1)
                    dve.wait_ge(y_read, e + 1)
                    step(nc.vector.tensor_tensor(now, now, bias0[:, :, :].to_broadcast([P, ROW_BLOCKS, FEATURES]), ALU.add))
                    step(nc.vector.tensor_tensor(now, now, rows, ALU.add))
                elif layer == CONCAT:
                    nc.vector.tensor_tensor(now, y_rows, bias1[:, :, :].to_broadcast([P, ROW_BLOCKS, FEATURES]),
                                            ALU.add).then_inc(y_read, 1)
                    dve.wait_ge(y_read, e + 1)
                    step(nc.vector.scalar_tensor_tensor(out=now, in0=now, scalar=0.0, in1=rows, op0=ALU.max, op1=ALU.add))
                else:
                    step(nc.vector.tensor_tensor(now, y_rows, by_row(inv_degree[:, ds(ROW_BLOCKS * c, ROW_BLOCKS)]), ALU.mult))
                    nc.vector.tensor_tensor(now, now, y_self_rows, ALU.add).then_inc(y_read, 1)
                    dve.wait_ge(y_read, e + 1)
                    step(nc.vector.tensor_tensor(now, now, rows, ALU.add))
                statistics(e, step)

                def rest():
                    normalize(e, c, step)
                    assert done[0] == steps_of[layer], (layer, done[0])
                return rest

            def chunk(layer, c, before, last_c):
                rest = None
                for n in range(PAIRS):
                    turn(layer, c, n)
                    if n == 5 and before is not None:
                        rest = combine(before, last_c)
                    if n == 6 and rest:
                        rest()
                    if layer == DEGREE and n in (6, 10, 14):
                        sum_tile(c, n // 4 - 1)
                if layer == DEGREE:
                    sum_tile(c, TILES - 1)
                    sum_rows(c)

            dve.wait_ge(rows_loaded, 16)
            dve.wait_ge(constants_loaded, 16 * 11)
            chunk(DEGREE, 0, None, None)
            with dve.Fori(1, CHUNKS) as c:
                chunk(DEGREE, c, DEGREE, c - 1)
            for layer in (CONCAT, BATCHNORM):
                chunk(layer, 0, layer - 1, CHUNKS - 1)
                with dve.Fori(1, CHUNKS) as c:
                    chunk(layer, c, layer, c - 1)

            for n in range(4):
                turn(SAGE, 0, n)
            combine(BATCHNORM, CHUNKS - 1)
            step, done = stepper(first_step[BATCHNORM])
            dve.wait_ge(bn_counted, CHUNKS)
            nc.vector.bn_aggr(bn_mean_var[:, :], bn_stats[:, :, :].rearrange("p c s -> p (c s)")).then_inc(bn_counted, 1)
            dve.wait_ge(bn_counted, CHUNKS + 1)
            nc.vector.tensor_scalar(bn_var_eps[:, :], bn_mean_var[:, 1:2], EPS, None, ALU.add).then_inc(bn_var_ready, 1)
            dve.wait_ge(bn_std_ready, 1)
            refine(step, bn_rstd[:, :], bn_std[:, :], bn_var_eps[:, :], bn_newton[:, :])
            step(nc.vector.tensor_tensor(bn_scale[:, :], gamma2[:, :], bn_rstd[:, :], ALU.mult))
            step(nc.vector.tensor_tensor(bn_newton[:, :], bn_mean_var[:, 0:1], bn_scale[:, :], ALU.mult))
            nc.vector.tensor_tensor(bn_shift[:, :], beta2[:, :], bn_newton[:, :], ALU.subtract).then_inc(bn_ready, 1)

            def finish_batchnorm(t):
                for c in (2 * t, 2 * t + 1):
                    dve.wait_ge(affine_done, c + 1)
                    if c >= 2:
                        dve.wait_ge(h_back, c - 1)
                    nc.vector.scalar_tensor_tensor(out=leaky[:, c % 2, :], in0=h_t[:, c, :], scalar=SLOPE,
                                                   in1=h_t[:, c, :], op0=ALU.mult,
                                                   op1=ALU.max).then_inc(leaky_done, 1)
                for c in (2 * t, 2 * t + 1):
                    e = CHUNKS * BATCHNORM + c
                    dve.wait_ge(h_back, c + 1)
                    dve.wait_ge(x_normed, e - c % 2)
                    step(nc.vector.tensor_tensor(new[:, c % 2], h_turned[:, c % 2, :].rearrange("p (b d) -> p b d", b=ROW_BLOCKS),
                                                 x_rows[:, ROW_BLOCKS * c:ROW_BLOCKS * (c + 1), :], ALU.add))
                    statistics(e, step, c % 2)
                for c in (2 * t, 2 * t + 1):
                    normalize(CHUNKS * BATCHNORM + c, c, step, c % 2)

            finish_batchnorm(0)
            finish_batchnorm(1)
            for n in range(4, 8):
                turn(SAGE, 0, n)
            finish_batchnorm(2)
            for n in range(8, 12):
                turn(SAGE, 0, n)
            finish_batchnorm(3)
            assert first_step[BATCHNORM] + done[0] == first_step[SAGE], done[0]
            for n in range(12, PAIRS):
                turn(SAGE, 0, n)
            with dve.Fori(1, CHUNKS) as c:
                chunk(SAGE, c, SAGE, c - 1)
            rest = combine(SAGE, CHUNKS - 1)
            rest()

        @block.tensor
        def _(pe):
            pe.wait_ge(identity_made, 1 + QUADRANTS)
            pe.wait_ge(constants_loaded, 16 * 11)
            for a in range(2):
                last = nc.tensor.transpose(x_turned[:, FEATURES * a:FEATURES * (a + 1)],
                                           w1[:, FEATURES * a:FEATURES * (a + 1)], ident[:, :])
            last.then_inc(w1_turned, 1)
            pe.wait_ge(w1_copied, 1)

            def multiply(layer, c, n):
                k = CHUNKS * layer + c
                first = is_number(c) and c == 0
                into = agg[:, 0, :] if first else agg[:, ds(c % 2, 1), :].rearrange("p a n -> p (a n)")
                if layer == DEGREE or n not in SPLIT:
                    if first and layer == DEGREE and n % TILE_PAIRS == 0:
                        pe.wait_ge(blocks_loaded[n // TILE_PAIRS], LOAD)
                    elif first and layer > DEGREE:
                        pe.wait_ge(operand_high, PAIRS * (layer - 1) + n + 1)
                    pe.wait_ge(pair_turned, PAIRS * k + n + 1)
                    for b in range(2):
                        last = nc.tensor.matmul(into, x_blocks[:, 2 * n + b, :], turned[:, n % RING, b, :],
                                                start=n == 0 and b == 0, stop=n == PAIRS - 1 and b == 1)
                else:
                    s = SPLIT.index(n)
                    if first:
                        pe.wait_ge(operand_low, SPLITS * (layer - 1) + s + 1)
                    pe.wait_ge(high_ready, SPLITS * (k - CHUNKS) + s + 1)
                    for b in range(2):
                        for part in (x_high, x_low):
                            nc.tensor.matmul(into, part[:, s, b, :], high[:, s % PART_RING, b, :],
                                             start=False, stop=False)
                    pe.wait_ge(low_ready, SPLITS * (k - CHUNKS) + s + 1)
                    for b in range(2):
                        last = nc.tensor.matmul(into, x_high[:, s, b, :], low[:, s % PART_RING, b, :],
                                                start=False, stop=False)
                last.then_inc(pair_used, 1)

            def own_rows(layer, c):
                if layer == DEGREE:
                    into = agg[:, 0, :] if is_number(c) else agg[:, ds(c % 2, 1), :].rearrange("p a n -> p (a n)")
                    pe.wait_ge(loops_made, c + 1)
                    for b in range(ROW_BLOCKS):
                        last = nc.tensor.matmul(into[:, P * b:P * (b + 1)], x_chunk[:, b, :], loops[:, b, :],
                                                start=False, stop=False)
                    last.then_inc(loops_added, 1)
                elif layer != BATCHNORM:
                    pe.wait_ge(chunk_staged, CHUNKS * (1 if layer == CONCAT else 2) + c + 1)
                    before = (0 if layer == CONCAT else CHUNKS) + c
                    if not (is_number(before) and before == 0):
                        pe.wait_ge(chunk_t_copied, before)
                    for b in range(ROW_BLOCKS):
                        last = nc.tensor.transpose(x_turned[:, P * b:P * (b + 1)], x_chunk[:, b, :], ident[:, :])
                    last.then_inc(chunk_turned, 1)

            def weights(layer, c):
                e = CHUNKS * layer + c
                if layer == DEGREE:
                    pe.wait_ge(rows_summed, c + 1)
                    grouped = row_sums[:, :].rearrange("p (b u) -> p b u", u=QUADRANTS)
                    for u in range(QUADRANTS):
                        at = QUAD * (QUADRANTS - 1 - u)
                        last = nc.tensor.matmul(sums[:, 0:ROW_BLOCKS], fold[:, at:at + P], grouped[:, :, u],
                                                start=u == 0, stop=u == QUADRANTS - 1)
                    last.then_inc(degree_done, 1)
                pe.wait_ge(agg_copied, e + 1)
                if not (is_number(e) and e == 0):
                    pe.wait_ge(y_read, e)
                if layer in (CONCAT, SAGE):
                    pe.wait_ge(chunk_t_copied, (0 if layer == CONCAT else CHUNKS) + c + 1)
                if layer == BATCHNORM:
                    last = nc.tensor.matmul(y[:, :], w2[:, :], agg_t[:, :], start=True, stop=True)
                for b in range(ROW_BLOCKS if layer != BATCHNORM else 0):
                    cols = slice(P * b, P * (b + 1))
                    if layer == DEGREE:
                        last = nc.tensor.matmul(y[:, cols], agg_t[:, cols], w0[:, :], start=True, stop=True)
                    elif layer == CONCAT:
                        nc.tensor.matmul(y[:, cols], x_chunk_t[:, cols], w1_t[:, 0, :], start=True, stop=False)
                        last = nc.tensor.matmul(y[:, cols], agg_t[:, cols], w1_t[:, 1, :], start=False, stop=True)
                    else:
                        nc.tensor.matmul(y_self[:, cols], x_chunk_t[:, cols], w3_self[:, :], start=True, stop=True)
                        last = nc.tensor.matmul(y[:, cols], agg_t[:, cols], w3_neighbour[:, :], start=True, stop=True)
                last.then_inc(y_done, 1)

            def chunk(layer, c, before, last_c):
                for n in range(PAIRS):
                    multiply(layer, c, n)
                    if n == 1 and before is not None:
                        weights(before, last_c)
                    if n == 12:
                        own_rows(layer, c)

            def back_to_rows(t):
                for c in (2 * t, 2 * t + 1):
                    pe.wait_ge(leaky_done, c + 1)
                    if c >= 2:
                        pe.wait_ge(var_ready, CHUNKS * BATCHNORM + c - 1)
                    for b in range(ROW_BLOCKS):
                        cols = slice(P * b, P * (b + 1))
                        last = nc.tensor.transpose(h_turned[:, c % 2, cols], leaky[:, c % 2, cols], ident[:, :])
                    last.then_inc(h_back, 1)

            for layer in (DEGREE, CONCAT, BATCHNORM):
                chunk(layer, 0, layer - 1 if layer else None, CHUNKS - 1)
                with pe.Fori(1, CHUNKS) as c:
                    chunk(layer, c, layer, c - 1)
            weights(BATCHNORM, CHUNKS - 1)
            back_to_rows(0)
            back_to_rows(1)
            for n in range(PAIRS):
                multiply(SAGE, 0, n)
                if n in (3, 7):
                    back_to_rows(n // 4 + 2)
                if n == 12:
                    own_rows(SAGE, 0)
            with pe.Fori(1, CHUNKS) as c:
                chunk(SAGE, c, SAGE, c - 1)
            weights(SAGE, CHUNKS - 1)


_INS = ["x", "adj", "L0_gnn_kernel", "L0_gnn_bias", "L0_gnn_beta", "L1_gnn_W", "L1_gnn_b", "L2_gnn_W", "L2_gnn_b",
        "L2_gnn_gamma", "L2_gnn_beta", "L3_gnn_W_self", "L3_gnn_W_neigh"]


def kernel(**inputs):
    import numpy as np
    import concourse.bacc as bacc
    from concourse.bass_utils import run_bass_kernel_spmd

    nc = bacc.Bacc("TRN2", target_bir_lowering=False, num_devices=1)
    arrays, args = {}, []
    for name in _INS:
        a = np.ascontiguousarray(inputs[name])
        arrays[f"in_{name}"] = a
        args.append(nc.dram_tensor(f"in_{name}", a.shape, mybir.dt.from_np(a.dtype), kind="ExternalInput").ap())
    args.append(nc.dram_tensor("out", (NODES, FEATURES), mybir.dt.float32, kind="ExternalOutput").ap())
    gnn_layers(nc, *args)
    return run_bass_kernel_spmd(nc, [arrays], core_ids=[0]).results[0]["out"]
```

```python
from contextlib import ExitStack

import concourse.bass as bass
from concourse import mybir

NODES, FEATURES, LAYERS = 4096, 128, 4
P = 128
QUADRANTS, QUAD = 4, 32
CHUNK = 512
CHUNKS = NODES // CHUNK
TILE_COLUMNS = 512
TILES = NODES // TILE_COLUMNS
QUAD_COLUMNS = TILE_COLUMNS // QUADRANTS
GROUPS = CHUNK // QUAD
BLOCKS = NODES // P
PAIRS = BLOCKS // 2
TILE_PAIRS = PAIRS // TILES
ROW_BLOCKS = CHUNK // P
QUARTERED = [0, 1, 2, 4, 5, 6]
QUARTERS = len(QUARTERED)
FIRST_RING = 4
SPLIT_RING, NATIVE_RING = 5, 3
RING = SPLIT_RING + NATIVE_RING
PART_RING = 3
PART_SLOT = [0, 1, 2, 0, 1, 2, 0, 1, 2, 1]
SPLIT = [1, 2, 4, 5, 7, 8, 10, 11, 13, 14]
SPLITS = len(SPLIT)
assert len(PART_SLOT) == SPLITS
NATIVE = [n for n in range(PAIRS) if n not in SPLIT]
DEGREE, CONCAT, BATCHNORM, SAGE = range(4)
OPERANDS_AFTER = {7: (0, 1), 11: (2, 3), 14: (4, 5)}
FIRST_OPERANDS = [(0, 1), (2, 3), (4, 5, 6)]
HIGH_AFTER = [(), (4,), (5,), (7, 8), (10,), (11,), (13,), (14,)]
EPS = 1e-5
SLOPE = 0.2
LOAD = 16 * QUADRANTS
LOOPS = 16 * (1 + ROW_BLOCKS)
CONSTANTS = 16 * 9


def is_number(value):
    return isinstance(value, int)


def slot_of(layer, n):
    if layer == 0:
        return n % FIRST_RING
    if n in SPLIT:
        return SPLIT.index(n) % SPLIT_RING
    return SPLIT_RING + NATIVE.index(n) % NATIVE_RING


def gnn_layers(nc, x, adj, w_degree, bias_degree, self_loop, w_concat, bias_concat, w_batch, bias_batch,
               gamma, shift_batch, w_self, w_neighbour, out):
    f32, f32r = mybir.dt.float32, mybir.dt.float32r
    ACT, ALU, AXIS = mybir.ActivationFunctionType, mybir.AluOpType, mybir.AxisListType
    ds = bass.ds

    adj_tiles = adj.rearrange("(c g r) (t q f) -> c t q r g f", g=GROUPS, r=QUAD, q=QUADRANTS, t=TILES)
    x_by_chunk = x.rearrange("(c q b j) d -> c q j b d", q=QUADRANTS, b=ROW_BLOCKS, j=QUAD)
    loops_by_block = self_loop.rearrange("(c q b j) -> b c q j", q=QUADRANTS, b=ROW_BLOCKS, j=QUAD)
    out_by_chunk = out.rearrange("(c q b j) d -> c q j b d", q=QUADRANTS, b=ROW_BLOCKS, j=QUAD)

    with ExitStack() as ctx:
        def sbuf(name, shape, dtype=f32):
            return ctx.enter_context(nc.sbuf_tensor(name, shape, dtype))

        def psum(name, shape):
            return ctx.enter_context(nc.psum_tensor(name, shape, f32))

        def sem(name):
            return ctx.enter_context(nc.semaphore(name))

        raw = sbuf("raw", [P, TILES, GROUPS, QUAD_COLUMNS])
        turned = sbuf("turned", [P, RING, 2, CHUNK])
        high = sbuf("high", [P, PART_RING, 2, CHUNK], f32r)
        low = sbuf("low", [P, PART_RING, 2, CHUNK], f32r)
        x_rows = sbuf("x_rows", [P, BLOCKS, FEATURES])
        x_blocks = sbuf("x_blocks", [P, BLOCKS, FEATURES])
        x_high = sbuf("x_high", [P, SPLITS, 2, FEATURES], f32r)
        x_low = sbuf("x_low", [P, SPLITS, 2, FEATURES], f32r)
        x_chunk = sbuf("x_chunk", [P, ROW_BLOCKS, FEATURES])
        x_chunk_t = sbuf("x_chunk_t", [P, CHUNK])
        agg_t = sbuf("agg_t", [P, CHUNK])
        four_relu = [x_chunk[:, :, :].rearrange("p b d -> p (b d)"), x_chunk_t[:, :]]
        w1 = x_chunk_t[:, 0:2 * FEATURES]
        h_t = sbuf("h_t", [P, CHUNKS, CHUNK])
        halves = [h_t[:, 2 * i:2 * i + 2, :].rearrange("p a (b c) -> p (a b) c", b=8) for i in range(3)]
        quarters = [h_t[:, 6 + i, :].rearrange("p (a c) -> p a c", a=GROUPS) for i in range(2)]
        loops = sbuf("loops", [P, ROW_BLOCKS, P])
        new = sbuf("new", [P, ROW_BLOCKS, FEATURES])
        stats = sbuf("stats", [P, 2, ROW_BLOCKS, 6])
        mean_var = sbuf("mean_var", [P, 2, ROW_BLOCKS, 2])
        var_eps = sbuf("var_eps", [P, 2, ROW_BLOCKS])
        std = sbuf("std", [P, 2, ROW_BLOCKS])
        rstd = sbuf("rstd", [P, 2, ROW_BLOCKS])
        newton = sbuf("newton", [P, 2, ROW_BLOCKS])
        minus_mean = sbuf("minus_mean", [P, 2, ROW_BLOCKS])
        row_parts = sbuf("row_parts", [P, GROUPS, TILES])
        row_sums = sbuf("row_sums", [P, GROUPS])
        degree = sbuf("degree", [P, ROW_BLOCKS])
        inv_looped = sbuf("inv_looped", [P, ROW_BLOCKS])
        inv_degree = sbuf("inv_degree", [P, BLOCKS])
        bn_stats = sbuf("bn_stats", [P, CHUNKS, 6])
        bn_mean_var = sbuf("bn_mean_var", [P, 2])
        bn_var_eps = sbuf("bn_var_eps", [P, 1])
        bn_std = sbuf("bn_std", [P, 1])
        bn_rstd = sbuf("bn_rstd", [P, 1])
        bn_newton = sbuf("bn_newton", [P, 1])
        bn_scale = sbuf("bn_scale", [P, 1])
        bn_shift = sbuf("bn_shift", [P, 1])
        ident = sbuf("ident", [P, P])
        fifth = sbuf("fifth", [P, P])
        fold = sbuf("fold", [P, 3 * QUAD + P])
        loop_rows = sbuf("loop_rows", [P, BLOCKS])
        loops_raw = sbuf("loops_raw", [BLOCKS, P])
        w0 = sbuf("w0", [P, FEATURES])
        w1_t = sbuf("w1_t", [P, 2, FEATURES])
        w2 = sbuf("w2", [P, FEATURES])
        w3_self = sbuf("w3_self", [P, FEATURES])
        w3_neighbour = sbuf("w3_neighbour", [P, FEATURES])
        bias0 = sbuf("bias0", [P, 1, FEATURES])
        bias1 = sbuf("bias1", [P, 1, FEATURES])
        bias2 = sbuf("bias2", [P, 1])
        gamma2 = sbuf("gamma2", [P, 1])
        beta2 = sbuf("beta2", [P, 1])
        agg = psum("agg", [P, 2, CHUNK])
        y = psum("y", [P, CHUNK])
        y_self = psum("y_self", [P, CHUNK])
        x_turned = psum("x_turned", [P, CHUNK])
        sums = psum("sums", [P, CHUNK])
        h_turned = psum("h_turned", [P, 2, CHUNK])
        y_rows = y[:, :].rearrange("p (b d) -> p b d", b=ROW_BLOCKS)
        y_self_rows = y_self[:, :].rearrange("p (b d) -> p b d", b=ROW_BLOCKS)

        def half_of(t):
            return halves[QUARTERED.index(t) % 2 if t in QUARTERED else 2]

        def quarter_of(t):
            return quarters[QUARTERED.index(t) % 2]

        tile_loaded = [sem(f"tile_loaded_{t}") for t in range(TILES)]
        blocks_copied = sem("blocks_copied")
        rows_loaded = [sem(f"rows_loaded_{c}") for c in range(CHUNKS)]
        loops_loaded, loops_placed = sem("loops_loaded"), sem("loops_placed")
        constants_loaded, fifth_made = sem("constants_loaded"), sem("fifth_made")
        self_made = sem("self_made")
        bits_made, identity_made = sem("bits_made"), sem("identity_made")
        w1_turned, w1_copied = sem("w1_turned"), sem("w1_copied")
        pair_turned, pair_used = sem("pair_turned"), sem("pair_used")
        high_ready, low_ready = sem("high_ready"), sem("low_ready")
        agg_copied, y_done, y_read = sem("agg_copied"), sem("y_done"), sem("y_read")
        chunk_staged, loops_made, loops_added = sem("chunk_staged"), sem("loops_made"), sem("loops_added")
        chunk_turned, chunk_t_copied = sem("chunk_turned"), sem("chunk_t_copied")
        half_folded, quarter_folded = sem("half_folded"), sem("quarter_folded")
        tile_summed, rows_summed, degree_done = sem("tile_summed"), sem("rows_summed"), sem("degree_done")
        var_ready, std_ready, norm_ready = sem("var_ready"), sem("std_ready"), sem("norm_ready")
        x_normed, y_scaled, inv_ready = sem("x_normed"), sem("y_scaled"), sem("inv_ready")
        operand_high, operand_low = sem("operand_high"), sem("operand_low")
        bn_counted = sem("bn_counted")
        bn_var_ready, bn_std_ready, bn_ready = sem("bn_var_ready"), sem("bn_std_ready"), sem("bn_ready")
        affine_done, relu_done, h_back = sem("affine_done"), sem("relu_done"), sem("h_back")
        vector_step, stored = sem("vector_step"), sem("stored")
        block = ctx.enter_context(nc.Block())

        @block.sync
        def _(sp):
            def load(layer, c, t):
                k = CHUNKS * layer + c
                if not (is_number(k) and k == 0):
                    if layer == DEGREE or is_number(c) and c == 0 and layer == CONCAT:
                        sp.wait_ge(tile_summed, TILES * (k - 1) + t + 1)
                    else:
                        sp.wait_ge(pair_turned, PAIRS * (k - 1) + TILE_PAIRS * (t + 1))
                for q in (0, 2, 1, 3):
                    lanes = slice(QUAD * q, QUAD * (q + 1))
                    if is_number(c):
                        source = adj_tiles[c, t, q]
                    else:
                        source = adj_tiles[ds(c, 1), t, q].rearrange("a r g f -> (a r) g f")
                    sp.dma_start(raw[lanes, t, :, :], source).then_inc(tile_loaded[t], 16)

            def store(c):
                sp.wait_ge(x_normed, CHUNKS * SAGE + c + 1)
                for q in range(QUADRANTS):
                    if is_number(c):
                        target = out_by_chunk[c, q]
                    else:
                        target = out_by_chunk[ds(c, 1), q].rearrange("a j b d -> (a j) b d")
                    sp.dma_start(target, x_rows[QUAD * q:QUAD * (q + 1), ds(ROW_BLOCKS * c, ROW_BLOCKS), :],
                                 ).then_inc(stored, 16)

            for layer in range(LAYERS):
                for c in (0, 1):
                    for t in range(TILES):
                        load(layer, c, t)
                        if layer == DEGREE and c == 0:
                            for q in range(QUADRANTS):
                                sp.dma_start(x_rows[QUAD * q:QUAD * (q + 1), ROW_BLOCKS * t:ROW_BLOCKS * (t + 1), :],
                                             x_by_chunk[t, q]).then_inc(rows_loaded[t], 16)
                with sp.Fori(2, CHUNKS) as c:
                    for t in range(TILES):
                        load(layer, c, t)
                    if layer == SAGE:
                        store(c - 2)
            store(CHUNKS - 2)
            store(CHUNKS - 1)
            sp.wait_ge(stored, 16 * QUADRANTS * CHUNKS)

        @block.gpsimd
        def _(pool):
            nc.gpsimd.memset(ident[:, :], 0.0).then_inc(bits_made, 1)
            nc.gpsimd.memset(fold[:, :], 0.0).then_inc(bits_made, 1)
            pool.wait_ge(bits_made, 2)
            nc.gpsimd.affine_select(out=ident[:, :], in_=ident[:, :], compare_op=ALU.not_equal, fill=1.0,
                                    base=0, pattern=[[-1, P]], channel_multiplier=1).then_inc(identity_made, 1)
            pool.wait_ge(identity_made, 1)
            nc.gpsimd.tensor_scalar(fifth[:, :], ident[:, :], SLOPE, None, ALU.mult).then_inc(fifth_made, 1)
            middle = fold[:, 3 * QUAD:4 * QUAD]
            for q in range(QUADRANTS):
                nc.gpsimd.tensor_tensor(middle, middle, ident[:, QUAD * q:QUAD * (q + 1)],
                                        ALU.add).then_inc(identity_made, 1)
                pool.wait_ge(identity_made, q + 2)

            def fold_half(c, t):
                pool.wait_ge(tile_loaded[t], LOAD * (c + 1))
                if t in QUARTERED:
                    i = QUARTERED.index(t)
                    if not (is_number(c) and c == 0 and i < 2):
                        pool.wait_ge(quarter_folded, QUARTERS * c + i - 1)
                elif not (is_number(c) and c == 0 and t < TILES // 2):
                    pool.wait_ge(tile_summed, TILES * c + t - TILES // 2 + 1)
                nc.gpsimd.tensor_tensor(half_of(t), raw[:, t, :, 0:QUAD_COLUMNS // 2],
                                        raw[:, t, :, QUAD_COLUMNS // 2:QUAD_COLUMNS],
                                        ALU.add).then_inc(half_folded, 1)

            def fold_quarter(c, t):
                i = QUARTERED.index(t)
                pool.wait_ge(half_folded, TILES * c + t + 1)
                if i >= 2:
                    pool.wait_ge(tile_summed, TILES * c + QUARTERED[i - 2] + 1)
                elif not (is_number(c) and c == 0):
                    pool.wait_ge(tile_summed, TILES * (c - 1) + QUARTERED[i - 2] + 1)
                nc.gpsimd.tensor_tensor(quarter_of(t), half_of(t)[:, :, 0:QUAD_COLUMNS // 4],
                                        half_of(t)[:, :, QUAD_COLUMNS // 4:QUAD_COLUMNS // 2],
                                        ALU.add).then_inc(quarter_folded, 1)

            def fold_tile(c, t):
                fold_half(c, t)
                if t - 1 in QUARTERED:
                    fold_quarter(c, t - 1)

            def low_part(layer, c, n):
                s = SPLIT.index(n)
                pool.wait_ge(high_ready, SPLITS * (CHUNKS * (layer - 1) + c) + s + 1)
                nc.gpsimd.tensor_tensor(low[:, PART_SLOT[s]], turned[:, slot_of(layer, n)],
                                        high[:, PART_SLOT[s]].bitcast(f32),
                                        ALU.subtract).then_inc(low_ready, 1)

            def low_operand(layer, n):
                s = SPLIT.index(n)
                pool.wait_ge(operand_high, PAIRS * (layer - 1) + n + 1)
                nc.gpsimd.tensor_tensor(x_low[:, s], x_rows[:, 2 * n:2 * n + 2, :], x_high[:, s].bitcast(f32),
                                        ALU.subtract).then_inc(operand_low, 1)

            def low_operands(layer, *chunks):
                for n in SPLIT:
                    if n // TILE_PAIRS in chunks:
                        low_operand(layer, n)

            for t in range(TILES):
                fold_tile(0, t)
            with pool.Fori(1, CHUNKS - 1) as c:
                for t in range(TILES):
                    fold_tile(c, t)
            for t in range(TILES):
                fold_tile(CHUNKS - 1, t)
                if t >= 5:
                    low_operands(CONCAT, *FIRST_OPERANDS[t - 5])
            pool.wait_ge(constants_loaded, CONSTANTS)
            nc.gpsimd.tensor_tensor(w3_self[:, :], w3_self[:, :], ident[:, :], ALU.add).then_inc(self_made, 1)
            for layer in range(1, LAYERS):
                if layer - 1 != BATCHNORM:
                    for n in SPLIT:
                        low_part(layer, 0, n)
                        if n == 10:
                            low_operands(layer, CHUNKS - 1)
                else:
                    low_part(layer, 0, 1)
                    low_part(layer, 0, 2)
                    for m in range(CHUNKS):
                        low_operands(layer, m)
                        for n in HIGH_AFTER[m]:
                            low_part(layer, 0, n)
                with pool.Fori(1, CHUNKS - 1) as c:
                    for n in SPLIT:
                        low_part(layer, c, n)
                for n in SPLIT:
                    low_part(layer, CHUNKS - 1, n)
                    if layer < BATCHNORM and n in OPERANDS_AFTER:
                        low_operands(layer + 1, *OPERANDS_AFTER[n])
                if layer < BATCHNORM:
                    low_operands(layer + 1, CHUNKS - 2)

        @block.scalar
        def _(act):
            def lanes(q):
                return slice(QUAD * q, QUAD * (q + 1))

            act.wait_ge(tile_loaded[1], LOAD)
            for b in range(ROW_BLOCKS):
                act.dma_start(loops_raw[CHUNKS * b:CHUNKS * (b + 1), :].rearrange("c (q j) -> c q j", q=QUADRANTS),
                              loops_by_block[b]).then_inc(loops_loaded, 16)
            act.dma_start(w1, w_concat).then_inc(loops_loaded, 16)

            def load_constants():
                loads = [(w0[:, :], w_degree), (w2[:, :], w_batch), (w3_self[:, :], w_self),
                         (w3_neighbour[:, :], w_neighbour),
                         (bias0[:, 0, :], bias_degree.partition_broadcast(P)),
                         (bias1[:, 0, :], bias_concat.partition_broadcast(P))]
                loads += [(to[:, :], a.rearrange("(p a) -> p a", a=1))
                          for to, a in ((bias2, bias_batch), (gamma2, gamma), (beta2, shift_batch))]
                assert CONSTANTS == 16 * len(loads)
                for to, a in loads:
                    act.dma_start(to, a).then_inc(constants_loaded, 16)

            def high_part(layer, c, n):
                s = SPLIT.index(n)
                k = CHUNKS * layer + c
                act.wait_ge(pair_turned, PAIRS * k + n + 1)
                earlier = [i for i in range(s) if PART_SLOT[i] == PART_SLOT[s]]
                if earlier:
                    act.wait_ge(pair_used, PAIRS * k + SPLIT[earlier[-1]] + 1)
                elif not (is_number(k) and k == CHUNKS):
                    latest = max(i for i in range(SPLITS) if PART_SLOT[i] == PART_SLOT[s])
                    act.wait_ge(pair_used, PAIRS * (k - 1) + SPLIT[latest] + 1)
                nc.scalar.activation(high[:, PART_SLOT[s]], turned[:, slot_of(layer, n)],
                                     ACT.Copy).then_inc(high_ready, 1)

            def copy_agg(layer, c, parity):
                e = CHUNKS * layer + c
                act.wait_ge(pair_used, PAIRS * (e + 1))
                by_block = agg[:, ds(parity, 1), :].rearrange("p a (q b j) -> p (a b) q j", q=QUADRANTS, b=ROW_BLOCKS)
                nc.scalar.activation(agg_t[:, :].rearrange("p (b q j) -> p b q j", q=QUADRANTS, b=ROW_BLOCKS),
                                     by_block, ACT.Copy).then_inc(agg_copied, 1)

            def stage_chunk(layer, c):
                e = CHUNKS * layer + c
                if layer == DEGREE:
                    if is_number(c) and c == 0:
                        act.wait_ge(identity_made, 1)
                    else:
                        act.wait_ge(loops_added, c)
                else:
                    before = 0 if layer == CONCAT else CHUNKS
                    if is_number(c) and c == 0 and layer == CONCAT:
                        act.wait_ge(loops_added, CHUNKS)
                    else:
                        act.wait_ge(chunk_turned, before + c)
                    act.wait_ge(x_normed, e - CHUNKS + 1)
                nc.scalar.activation(x_chunk[:, :, :], x_rows[:, ds(ROW_BLOCKS * c, ROW_BLOCKS), :],
                                     ACT.Copy).then_inc(chunk_staged, 1)
                if layer == DEGREE:
                    for b in range(ROW_BLOCKS):
                        made = nc.scalar.activation(loops[:, b, :], ident[:, :], ACT.Copy,
                                                    scale=loop_rows[:, ds(ROW_BLOCKS * c + b, 1)])
                    made.then_inc(loops_made, 1)

            def copy_chunk_t(layer, c):
                n = (0 if layer == CONCAT else CHUNKS) + c
                act.wait_ge(chunk_turned, n + 1)
                act.wait_ge(y_done, CHUNKS * layer + c)
                nc.scalar.activation(x_chunk_t[:, :], x_turned[:, :], ACT.Copy).then_inc(chunk_t_copied, 1)

            def by_degree(layer, c):
                inverse = inv_looped if layer == DEGREE else inv_degree
                if layer == DEGREE:
                    act.wait_ge(inv_ready, c + 1)
                act.wait_ge(y_done, CHUNKS * layer + c + 1)
                for b in range(ROW_BLOCKS):
                    at = b if layer == DEGREE else ds(ROW_BLOCKS * c + b, 1)
                    scale = inverse[:, b:b + 1] if layer == DEGREE else inverse[:, at]
                    done = nc.scalar.activation(new[:, b, :], y_rows[:, b, :], ACT.Copy, scale=scale)
                done.then_inc(y_scaled, 1)

            def root(layer, c, parity=0):
                act.wait_ge(var_ready, CHUNKS * layer + c + 1)
                nc.scalar.activation(std[:, parity, :], var_eps[:, parity, :], ACT.Sqrt).then_inc(std_ready, 1)

            def normalize(layer, c, rows, parity=0):
                act.wait_ge(norm_ready, CHUNKS * layer + c + 1)
                for b in range(ROW_BLOCKS):
                    to = x_rows[:, ds(ROW_BLOCKS * c + b, 1), :].rearrange("p a d -> p (a d)")
                    done = nc.scalar.activation(to, rows[:, b, :], ACT.Identity, scale=rstd[:, parity, b:b + 1],
                                                bias=minus_mean[:, parity, b:b + 1])
                done.then_inc(x_normed, 1)

            def high_operands(layer, *chunks):
                for m in chunks:
                    act.wait_ge(x_normed, CHUNKS * (layer - 1) + m + 1)
                    act.wait_ge(pair_used, PAIRS * (CHUNKS * layer - 1) + TILE_PAIRS * (m + 1))
                    for n in range(TILE_PAIRS * m, TILE_PAIRS * (m + 1)):
                        to = x_high[:, SPLIT.index(n)] if n in SPLIT else x_blocks[:, 2 * n:2 * n + 2, :]
                        nc.scalar.activation(to, x_rows[:, 2 * n:2 * n + 2, :], ACT.Copy).then_inc(operand_high, 1)

            for m in range(CHUNKS):
                if m == 4:
                    act.wait_ge(loops_placed, 1)
                    nc.scalar.activation(loop_rows[:, :].rearrange("p (c b) -> p b c", b=ROW_BLOCKS),
                                         sums[:, 0:BLOCKS].rearrange("p (b c) -> p b c", b=ROW_BLOCKS),
                                         ACT.Copy).then_inc(loops_placed, 1)
                    act.wait_ge(loops_placed, 2)
                    stage_chunk(DEGREE, 0)
                act.wait_ge(rows_loaded[m], LOAD)
                rows = slice(ROW_BLOCKS * m, ROW_BLOCKS * (m + 1))
                nc.scalar.activation(x_blocks[:, rows, :], x_rows[:, rows, :], ACT.Copy).then_inc(blocks_copied, 1)
            load_constants()
            act.wait_ge(w1_turned, 1)
            nc.scalar.activation(w1_t[:, :, :], x_turned[:, 0:2 * FEATURES].rearrange("p (a b) -> p a b", a=2),
                                 ACT.Copy).then_inc(w1_copied, 1)
            act.wait_ge(constants_loaded, CONSTANTS)
            with act.Fori(1, CHUNKS - 1) as c:
                copy_agg(DEGREE, c - 1, (c + 1) % 2)
                stage_chunk(DEGREE, c)
                by_degree(DEGREE, c - 1)
                root(DEGREE, c - 1)
                normalize(DEGREE, c - 1, new)
            copy_agg(DEGREE, CHUNKS - 2, 0)
            stage_chunk(DEGREE, CHUNKS - 1)
            by_degree(DEGREE, CHUNKS - 2)
            high_operands(CONCAT, *FIRST_OPERANDS[0])
            root(DEGREE, CHUNKS - 2)
            high_operands(CONCAT, *FIRST_OPERANDS[1])
            normalize(DEGREE, CHUNKS - 2, new)
            high_operands(CONCAT, *FIRST_OPERANDS[2])

            def chunk(layer, c, before):
                first = is_number(c) and c == 0
                last = is_number(c) and not first and layer < BATCHNORM
                last_c = CHUNKS - 1 if first else c - 1
                high_part(layer, c, 1)
                high_part(layer, c, 2)
                copy_agg(before, last_c, 1 if first else (c + 1) % 2)
                if layer in (CONCAT, SAGE):
                    stage_chunk(layer, c)
                high_part(layer, c, 4)
                high_part(layer, c, 5)
                if before in (DEGREE, SAGE):
                    by_degree(before, last_c)
                high_part(layer, c, 7)
                if last:
                    high_operands(layer + 1, *OPERANDS_AFTER[7])
                high_part(layer, c, 8)
                if before != BATCHNORM:
                    root(before, last_c)
                high_part(layer, c, 10)
                if before != BATCHNORM:
                    normalize(before, last_c, new)
                if first:
                    high_operands(layer, CHUNKS - 1)
                high_part(layer, c, 11)
                if last:
                    high_operands(layer + 1, *OPERANDS_AFTER[11])
                high_part(layer, c, 13)
                high_part(layer, c, 14)
                if last:
                    high_operands(layer + 1, *OPERANDS_AFTER[14])
                if layer in (CONCAT, SAGE):
                    copy_chunk_t(layer, c)
                if last:
                    high_operands(layer + 1, CHUNKS - 2)

            for layer in (CONCAT, BATCHNORM):
                chunk(layer, 0, layer - 1)
                with act.Fori(1, CHUNKS - 1) as c:
                    chunk(layer, c, layer)
                chunk(layer, CHUNKS - 1, layer)

            high_part(SAGE, 0, 1)
            high_part(SAGE, 0, 2)
            copy_agg(BATCHNORM, CHUNKS - 1, 1)
            act.wait_ge(bn_var_ready, 1)
            nc.scalar.activation(bn_std[:, :], bn_var_eps[:, :], ACT.Sqrt).then_inc(bn_std_ready, 1)
            act.wait_ge(bn_ready, 1)

            def affine(m):
                nc.scalar.activation(h_t[:, m, :], h_t[:, m, :], ACT.Identity, bias=bn_shift[:, :],
                                     scale=bn_scale[:, :]).then_inc(affine_done, 1)
                act.wait_ge(affine_done, m + 1)
                if m >= 2:
                    act.wait_ge(h_back, m - 1)
                nc.scalar.activation(four_relu[m % 2], h_t[:, m, :], ACT.Relu, scale=4.0).then_inc(relu_done, 1)

            for m in range(3):
                affine(m)
            for m in range(CHUNKS):
                root(BATCHNORM, m, m % 2)
                if m + 3 < CHUNKS:
                    affine(m + 3)
                normalize(BATCHNORM, m, h_turned[:, m % 2, :].rearrange("p (b d) -> p b d", b=ROW_BLOCKS), m % 2)
                high_operands(SAGE, m)
                for n in HIGH_AFTER[m]:
                    high_part(SAGE, 0, n)
            act.wait_ge(h_back, CHUNKS)
            stage_chunk(SAGE, 0)
            copy_chunk_t(SAGE, 0)
            with act.Fori(1, CHUNKS) as c:
                chunk(SAGE, c, SAGE)
            copy_agg(SAGE, CHUNKS - 1, 1)
            by_degree(SAGE, CHUNKS - 1)
            root(SAGE, CHUNKS - 1)
            normalize(SAGE, CHUNKS - 1, new)

        @block.vector
        def _(dve):
            def turn(layer, c, n):
                k = CHUNKS * layer + c
                t, at = n // TILE_PAIRS, 2 * QUAD * (n % TILE_PAIRS)
                if n % TILE_PAIRS == 0:
                    dve.wait_ge(tile_loaded[t], LOAD * (k + 1))
                if layer == DEGREE:
                    if not (is_number(k) and k == 0 and n < FIRST_RING):
                        dve.wait_ge(pair_used, PAIRS * k + n - FIRST_RING + 1)
                else:
                    ring, kind = (SPLIT_RING, SPLIT) if n in SPLIT else (NATIVE_RING, NATIVE)
                    i = kind.index(n)
                    if i >= ring:
                        dve.wait_ge(pair_used, PAIRS * k + kind[i - ring] + 1)
                    elif is_number(k) and k == CHUNKS:
                        if slot_of(layer, n) < FIRST_RING:
                            dve.wait_ge(pair_used, PAIRS * k - FIRST_RING + slot_of(layer, n) + 1)
                    else:
                        dve.wait_ge(pair_used, PAIRS * (k - 1) + kind[i - ring] + 1)
                nc.vector.transpose(turned[:, slot_of(layer, n)].rearrange("p b (g r) -> p g b r", g=GROUPS),
                                    raw[:, t, :, at:at + 2 * QUAD].rearrange("p g (b j) -> p g b j", b=2),
                                    ).then_inc(pair_turned, 1)

            def sum_tile(c, t):
                dve.wait_ge(pair_turned, PAIRS * c + TILE_PAIRS * (t + 1))
                if t in QUARTERED:
                    dve.wait_ge(quarter_folded, QUARTERS * c + QUARTERED.index(t) + 1)
                else:
                    dve.wait_ge(half_folded, TILES * c + t + 1)
                if t == 0 and not is_number(c):
                    dve.wait_ge(rows_summed, c)
                nc.vector.tensor_reduce(row_parts[:, :, t], quarter_of(t) if t in QUARTERED else half_of(t),
                                        AXIS.X, ALU.add).then_inc(tile_summed, 1)

            def sum_rows(c):
                dve.wait_ge(tile_summed, TILES * (c + 1))
                if not is_number(c):
                    dve.wait_ge(degree_done, c)
                nc.vector.tensor_reduce(row_sums[:, :], row_parts[:, :, :], AXIS.X, ALU.add).then_inc(rows_summed, 1)

            statistics_steps, refine_steps = 2, 4
            norm_steps = statistics_steps + refine_steps
            steps_of = [3 + 1 + norm_steps, 1 + norm_steps, norm_steps, norm_steps]
            first_step = [0]
            for layer in range(SAGE):
                first_step.append(first_step[-1] + CHUNKS * steps_of[layer] + (layer == BATCHNORM) * (refine_steps + 2))

            def stepper(base):
                done = [0]

                def step(instruction):
                    done[0] += 1
                    instruction.then_inc(vector_step, 1)
                    dve.wait_ge(vector_step, base + done[0])
                return step, done

            def row_statistics(rows, step, parity=0):
                for b in range(ROW_BLOCKS):
                    last = nc.vector.bn_stats(stats[:, parity, b, :], rows[:, b, :])
                step(last)

            def row_variances(step, parity=0):
                nc.vector.memset(var_eps[:, parity, :], EPS)
                for b in range(ROW_BLOCKS):
                    last = nc.vector.bn_aggr(mean_var[:, parity, b, :], stats[:, parity, b, :])
                step(last)
                nc.vector.tensor_tensor(var_eps[:, parity, :], mean_var[:, parity, :, 1], var_eps[:, parity, :],
                                        ALU.add).then_inc(var_ready, 1)

            def refine(step, r, root_of, square, scratch):
                step(nc.vector.reciprocal(r, root_of))
                step(nc.vector.scalar_tensor_tensor(out=scratch, in0=r, scalar=-0.5, in1=square,
                                                    op0=ALU.mult, op1=ALU.mult))
                step(nc.vector.tensor_tensor(scratch, scratch, r, ALU.mult))
                step(nc.vector.scalar_tensor_tensor(out=r, in0=scratch, scalar=1.5, in1=r,
                                                    op0=ALU.add, op1=ALU.mult))

            def norm_factors(e, step, parity=0):
                dve.wait_ge(std_ready, e + 1)
                refine(step, rstd[:, parity, :], std[:, parity, :], var_eps[:, parity, :], newton[:, parity, :])
                nc.vector.scalar_tensor_tensor(out=minus_mean[:, parity, :], in0=mean_var[:, parity, :, 0],
                                               scalar=-1.0, in1=rstd[:, parity, :], op0=ALU.mult,
                                               op1=ALU.mult).then_inc(norm_ready, 1)

            def epilogue(layer, c):
                e = CHUNKS * layer + c
                step, done = stepper(first_step[layer] + steps_of[layer] * c)
                rows = x_rows[:, ds(ROW_BLOCKS * c, ROW_BLOCKS), :]

                def invert():
                    blocks = ds(ROW_BLOCKS * c, ROW_BLOCKS)
                    dve.wait_ge(degree_done, c + 1)
                    step(nc.vector.tensor_tensor(degree[:, :], sums[:, 0:ROW_BLOCKS], loop_rows[:, blocks], ALU.add))
                    nc.vector.reciprocal(inv_looped[:, :], degree[:, :]).then_inc(inv_ready, 1)
                    dve.wait_ge(inv_ready, c + 1)
                    step(nc.vector.tensor_scalar(degree[:, :], sums[:, 0:ROW_BLOCKS], 1.0, None, ALU.max))
                    step(nc.vector.reciprocal(inv_degree[:, blocks], degree[:, :]))

                def combine():
                    if layer == DEGREE:
                        dve.wait_ge(y_scaled, c + 1)
                        nc.vector.tensor_tensor(new[:, :, :], new[:, :, :],
                                                bias0[:, :, :].to_broadcast([P, ROW_BLOCKS, FEATURES]),
                                                ALU.add).then_inc(y_read, 1)
                        dve.wait_ge(y_read, e + 1)
                        step(nc.vector.tensor_tensor(new[:, :, :], new[:, :, :], rows, ALU.add))
                    elif layer == CONCAT:
                        dve.wait_ge(y_done, e + 1)
                        nc.vector.tensor_tensor(new[:, :, :], y_rows,
                                                bias1[:, :, :].to_broadcast([P, ROW_BLOCKS, FEATURES]),
                                                ALU.add).then_inc(y_read, 1)
                        dve.wait_ge(y_read, e + 1)
                        step(nc.vector.scalar_tensor_tensor(out=new[:, :, :], in0=new[:, :, :], scalar=0.0,
                                                            in1=rows, op0=ALU.max, op1=ALU.add))
                    elif layer == BATCHNORM:
                        dve.wait_ge(y_done, e + 1)
                        nc.vector.tensor_scalar(h_t[:, ds(c, 1), :].rearrange("p a n -> p (a n)"), y[:, :],
                                                bias2[:, 0:1], None, ALU.add).then_inc(y_read, 1)
                    else:
                        dve.wait_ge(y_scaled, CHUNKS + c + 1)
                        nc.vector.tensor_tensor(new[:, :, :], new[:, :, :], y_self_rows, ALU.add).then_inc(y_read, 1)

                def statistics():
                    if layer in (BATCHNORM, SAGE):
                        dve.wait_ge(y_read, e + 1)
                    if layer == BATCHNORM:
                        nc.vector.bn_stats(bn_stats[:, ds(c, 1), :].rearrange("p a n -> p (a n)"),
                                           h_t[:, ds(c, 1), :].rearrange("p a n -> p (a n)")).then_inc(bn_counted, 1)
                    else:
                        row_statistics(new, step)

                def variances():
                    if layer != BATCHNORM:
                        row_variances(step)

                def factors():
                    if layer != BATCHNORM:
                        norm_factors(e, step)
                        assert done[0] == steps_of[layer], (layer, done[0])

                return (invert if layer == DEGREE else None), combine, statistics, variances, factors

            def chunk(layer, c, before, last_c):
                invert, *parts = epilogue(before, last_c) if before is not None else [None]
                at = (9, 10, 11, 12)
                for n in range(PAIRS):
                    turn(layer, c, n)
                    if before == DEGREE and n in (1, 3):
                        sum_tile(last_c, TILES - 2 + n // TILE_PAIRS)
                        if n == 3:
                            sum_rows(last_c)
                    if n == at[0] - 2 and invert:
                        invert()
                    if n in at and parts:
                        parts[at.index(n)]()
                    if layer == DEGREE and n >= 5 and n % TILE_PAIRS == 1:
                        sum_tile(c, n // TILE_PAIRS - 2)

            chunk(DEGREE, 0, None, None)
            for c in range(CHUNKS):
                dve.wait_ge(rows_loaded[c], LOAD)
            dve.wait_ge(constants_loaded, CONSTANTS)
            dve.wait_ge(loops_placed, 2)
            with dve.Fori(1, CHUNKS) as c:
                chunk(DEGREE, c, DEGREE, c - 1)
            for layer in (CONCAT, BATCHNORM):
                chunk(layer, 0, layer - 1, CHUNKS - 1)
                with dve.Fori(1, CHUNKS) as c:
                    chunk(layer, c, layer, c - 1)

            for n in range(6):
                turn(SAGE, 0, n)
            _, combine, statistics, _, _ = epilogue(BATCHNORM, CHUNKS - 1)
            combine()
            statistics()
            step, done = stepper(first_step[BATCHNORM])
            dve.wait_ge(bn_counted, CHUNKS)
            nc.vector.bn_aggr(bn_mean_var[:, :], bn_stats[:, :, :].rearrange("p c s -> p (c s)")).then_inc(bn_counted, 1)
            dve.wait_ge(bn_counted, CHUNKS + 1)
            nc.vector.tensor_scalar(bn_var_eps[:, :], bn_mean_var[:, 1:2], EPS, None, ALU.add).then_inc(bn_var_ready, 1)
            dve.wait_ge(bn_std_ready, 1)
            refine(step, bn_rstd[:, :], bn_std[:, :], bn_var_eps[:, :], bn_newton[:, :])
            step(nc.vector.tensor_tensor(bn_scale[:, :], gamma2[:, :], bn_rstd[:, :], ALU.mult))
            step(nc.vector.tensor_tensor(bn_newton[:, :], bn_mean_var[:, 0:1], bn_scale[:, :], ALU.mult))
            nc.vector.tensor_tensor(bn_shift[:, :], beta2[:, :], bn_newton[:, :], ALU.subtract).then_inc(bn_ready, 1)

            def chunk_statistics(m):
                dve.wait_ge(h_back, m + 1)
                row_statistics(h_turned[:, m % 2, :].rearrange("p (b d) -> p b d", b=ROW_BLOCKS), step, m % 2)
                row_variances(step, m % 2)

            chunk_statistics(0)
            for m in range(CHUNKS):
                if m + 1 < CHUNKS:
                    chunk_statistics(m + 1)
                norm_factors(CHUNKS * BATCHNORM + m, step, m % 2)
                if m >= 2 and 2 * m + 3 < PAIRS:
                    turn(SAGE, 0, 2 * m + 2)
                    turn(SAGE, 0, 2 * m + 3)
            assert first_step[BATCHNORM] + done[0] == first_step[SAGE], done[0]
            with dve.Fori(1, CHUNKS) as c:
                chunk(SAGE, c, SAGE, c - 1)
            for part in epilogue(SAGE, CHUNKS - 1)[1:]:
                part()

        @block.tensor
        def _(pe):
            def multiply(layer, c, n):
                k = CHUNKS * layer + c
                first = is_number(c) and c == 0
                into = agg[:, 0, :] if first else agg[:, ds(c % 2, 1), :].rearrange("p a n -> p (a n)")
                if layer == DEGREE or n not in SPLIT:
                    operands = x_blocks
                    if first and layer == DEGREE:
                        operands = x_rows
                        if n % TILE_PAIRS == 0:
                            pe.wait_ge(rows_loaded[n // TILE_PAIRS], LOAD)
                    elif first and layer > DEGREE:
                        pe.wait_ge(operand_high, PAIRS * (layer - 1) + n + 1)
                    pe.wait_ge(pair_turned, PAIRS * k + n + 1)
                    for b in range(2):
                        last = nc.tensor.matmul(into, operands[:, 2 * n + b, :], turned[:, slot_of(layer, n), b, :],
                                                start=n == 0 and b == 0, stop=n == PAIRS - 1 and b == 1)
                else:
                    s = SPLIT.index(n)
                    if first:
                        pe.wait_ge(operand_low, SPLITS * (layer - 1) + s + 1)
                    pe.wait_ge(high_ready, SPLITS * (k - CHUNKS) + s + 1)
                    for b in range(2):
                        for part in (x_high[:, s], x_low[:, s]):
                            nc.tensor.matmul(into, part[:, b, :], high[:, PART_SLOT[s], b, :],
                                             start=False, stop=False)
                    pe.wait_ge(low_ready, SPLITS * (k - CHUNKS) + s + 1)
                    for b in range(2):
                        last = nc.tensor.matmul(into, x_high[:, s, b, :], low[:, PART_SLOT[s], b, :],
                                                start=False, stop=False)
                last.then_inc(pair_used, 1)

            def place_loops():
                pe.wait_ge(loops_loaded, LOOPS)
                pe.wait_ge(identity_made, 1)
                nc.tensor.transpose(sums[:, 0:BLOCKS], loops_raw[:, :],
                                    ident[0:BLOCKS, 0:BLOCKS]).then_inc(loops_placed, 1)

            def own_rows(layer, c):
                if layer == DEGREE:
                    into = agg[:, ds(c % 2, 1), :].rearrange("p a (q b j) -> p (a b) q j", q=QUADRANTS, b=ROW_BLOCKS)
                    if is_number(c) and c == 0:
                        pe.wait_ge(identity_made, 1 + QUADRANTS)
                        pe.wait_ge(fifth_made, 1)
                        for a in range(2):
                            last = nc.tensor.transpose(x_turned[:, FEATURES * a:FEATURES * (a + 1)],
                                                       w1[:, FEATURES * a:FEATURES * (a + 1)], ident[:, :])
                        last.then_inc(w1_turned, 1)
                    pe.wait_ge(loops_made, c + 1)
                    for b in range(ROW_BLOCKS):
                        last = nc.tensor.matmul(into[:, b], x_chunk[:, b, :],
                                                loops[:, b, :].rearrange("p (q j) -> p q j", q=QUADRANTS),
                                                start=False, stop=False)
                    last.then_inc(loops_added, 1)
                elif layer != BATCHNORM:
                    pe.wait_ge(chunk_staged, CHUNKS * (1 if layer == CONCAT else 2) + c + 1)
                    before = (0 if layer == CONCAT else CHUNKS) + c
                    if not (is_number(before) and before == 0):
                        pe.wait_ge(chunk_t_copied, before)
                    else:
                        pe.wait_ge(w1_copied, 1)
                    for b in range(ROW_BLOCKS):
                        last = nc.tensor.transpose(x_turned[:, P * b:P * (b + 1)], x_chunk[:, b, :], ident[:, :])
                    last.then_inc(chunk_turned, 1)

            def weights(layer, c):
                e = CHUNKS * layer + c
                if layer == DEGREE:
                    pe.wait_ge(rows_summed, c + 1)
                    grouped = row_sums[:, :].rearrange("p (u b) -> p b u", u=QUADRANTS)
                    for u in range(QUADRANTS):
                        at = QUAD * (QUADRANTS - 1 - u)
                        last = nc.tensor.matmul(sums[:, 0:ROW_BLOCKS], fold[:, at:at + P], grouped[:, :, u],
                                                start=u == 0, stop=u == QUADRANTS - 1)
                    last.then_inc(degree_done, 1)
                pe.wait_ge(agg_copied, e + 1)
                if is_number(e) and e > 0 and c == CHUNKS - 1 and layer == SAGE:
                    pe.wait_ge(y_read, e)
                if layer in (CONCAT, SAGE):
                    pe.wait_ge(chunk_t_copied, (0 if layer == CONCAT else CHUNKS) + c + 1)
                if layer == BATCHNORM:
                    last = nc.tensor.matmul(y[:, :], w2[:, :], agg_t[:, :], start=True, stop=True)
                for b in range(ROW_BLOCKS if layer != BATCHNORM else 0):
                    cols = slice(P * b, P * (b + 1))
                    if layer == DEGREE:
                        last = nc.tensor.matmul(y[:, cols], agg_t[:, cols], w0[:, :], start=True, stop=True)
                    elif layer == CONCAT:
                        nc.tensor.matmul(y[:, cols], x_chunk_t[:, cols], w1_t[:, 0, :], start=True, stop=False)
                        last = nc.tensor.matmul(y[:, cols], agg_t[:, cols], w1_t[:, 1, :], start=False, stop=True)
                    else:
                        nc.tensor.matmul(y_self[:, cols], x_chunk_t[:, cols], w3_self[:, :], start=True, stop=True)
                        last = nc.tensor.matmul(y[:, cols], agg_t[:, cols], w3_neighbour[:, :], start=True, stop=True)
                last.then_inc(y_done, 1)

            def chunk(layer, c, before, last_c):
                for n in range(PAIRS):
                    multiply(layer, c, n)
                    if is_number(c) and c == 0 and layer == DEGREE and n == 7:
                        place_loops()
                    if before is not None and n == (3 if before == DEGREE else 1):
                        weights(before, last_c)
                    if n == 12:
                        own_rows(layer, c)

            def back_to_rows(m):
                for c in (m,):
                    pe.wait_ge(relu_done, c + 1)
                    if c >= 2:
                        pe.wait_ge(x_normed, CHUNKS * BATCHNORM + c - 1)
                    nc.tensor.matmul(h_turned[:, c % 2, :], ident[:, :],
                                     x_rows[:, ROW_BLOCKS * c:ROW_BLOCKS * (c + 1), :].rearrange("p b d -> p (b d)"),
                                     start=True, stop=False)
                    for b in range(ROW_BLOCKS):
                        cols = slice(P * b, P * (b + 1))
                        nc.tensor.matmul(h_turned[:, c % 2, cols], h_t[:, c, cols], fifth[:, :],
                                         start=False, stop=False)
                        last = nc.tensor.matmul(h_turned[:, c % 2, cols], four_relu[c % 2][:, cols], fifth[:, :],
                                                start=False, stop=b == ROW_BLOCKS - 1)
                    last.then_inc(h_back, 1)

            for layer in (DEGREE, CONCAT, BATCHNORM):
                chunk(layer, 0, layer - 1 if layer else None, CHUNKS - 1)
                if layer == DEGREE:
                    pe.wait_ge(blocks_copied, CHUNKS)
                with pe.Fori(1, CHUNKS) as c:
                    chunk(layer, c, layer, c - 1)
            weights(BATCHNORM, CHUNKS - 1)
            for m in range(3):
                back_to_rows(m)
            for n in range(PAIRS):
                multiply(SAGE, 0, n)
                if n % TILE_PAIRS and n // TILE_PAIRS + 3 < CHUNKS:
                    back_to_rows(n // TILE_PAIRS + 3)
                if n == 12:
                    own_rows(SAGE, 0)
            pe.wait_ge(self_made, 1)
            with pe.Fori(1, CHUNKS) as c:
                chunk(SAGE, c, SAGE, c - 1)
            weights(SAGE, CHUNKS - 1)


_INS = ["x", "adj", "L0_gnn_kernel", "L0_gnn_bias", "L0_gnn_beta", "L1_gnn_W", "L1_gnn_b", "L2_gnn_W", "L2_gnn_b",
        "L2_gnn_gamma", "L2_gnn_beta", "L3_gnn_W_self", "L3_gnn_W_neigh"]


def kernel(**inputs):
    import numpy as np
    import concourse.bacc as bacc
    from concourse.bass_utils import run_bass_kernel_spmd

    nc = bacc.Bacc("TRN2", target_bir_lowering=False, num_devices=1)
    arrays, args = {}, []
    for name in _INS:
        a = np.ascontiguousarray(inputs[name])
        arrays[f"in_{name}"] = a
        args.append(nc.dram_tensor(f"in_{name}", a.shape, mybir.dt.from_np(a.dtype), kind="ExternalInput").ap())
    args.append(nc.dram_tensor("out", (NODES, FEATURES), mybir.dt.float32, kind="ExternalOutput").ap())
    gnn_layers(nc, *args)
    return run_bass_kernel_spmd(nc, [arrays], core_ids=[0]).results[0]["out"]
```

```python
from contextlib import ExitStack

import concourse.bass as bass
from concourse import mybir

NODES, FEATURES, LAYERS = 4096, 128, 4
P = 128
QUADRANTS, QUAD = 4, 32
CHUNK = 512
CHUNKS = NODES // CHUNK
TILE_COLUMNS = 512
TILES = NODES // TILE_COLUMNS
QUAD_COLUMNS = TILE_COLUMNS // QUADRANTS
GROUPS = CHUNK // QUAD
BLOCKS = NODES // P
PAIRS = BLOCKS // 2
TILE_PAIRS = PAIRS // TILES
ROW_BLOCKS = CHUNK // P
QUARTERED = [0, 1, 2, 4, 5, 6]
QUARTERS = len(QUARTERED)
FIRST_RING = 4
SPLIT_RING, NATIVE_RING, PART_RING = 4, 2, 4
RING = SPLIT_RING + NATIVE_RING
SPLIT = [1, 2, 3, 5, 6, 7, 9, 10, 11, 13, 14, 15]
SPLITS = len(SPLIT)
VECTOR_LOW = {2: 4, 10: 12}
EARLY_LOW, LATE_LOW = VECTOR_LOW
GPSIMD_LOW = [n for n in SPLIT if n not in VECTOR_LOW]
NATIVE = [n for n in range(PAIRS) if n not in SPLIT]
DEGREE, CONCAT, BATCHNORM, SAGE = range(4)
OPERANDS_AFTER = {7: (0, 1), 11: (2, 3), 13: (4, 5)}
FIRST_OPERANDS = [(0, 1), (2, 3), (4, 5, 6)]
HIGH_BEFORE, HIGH_AFTER = (1, 2, 3, 5), [(), (6,), (7,), (9, 10), (11,), (13,), (14,), (15,)]
TURNED_BEFORE, TURNED_AFTER = (range(0, 6), range(6, 8)), [(), (8, 9), (10,), (11,), (12,), (13,), (14,), (15,)]
EPS = 1e-5
SLOPE = 0.2
LOAD = 16 * QUADRANTS
LOOPS = 16 * (1 + ROW_BLOCKS)
CONSTANTS = 16 * 9


def is_number(value):
    return isinstance(value, int)


def slot_of(layer, n):
    if layer == 0:
        return n % FIRST_RING
    if n in SPLIT:
        return SPLIT.index(n) % SPLIT_RING
    return SPLIT_RING + NATIVE.index(n) % NATIVE_RING


def gnn_layers(nc, x, adj, w_degree, bias_degree, self_loop, w_concat, bias_concat, w_batch, bias_batch,
               gamma, shift_batch, w_self, w_neighbour, out):
    f32, f32r = mybir.dt.float32, mybir.dt.float32r
    ACT, ALU, AXIS = mybir.ActivationFunctionType, mybir.AluOpType, mybir.AxisListType
    ds = bass.ds

    adj_tiles = adj.rearrange("(c g r) (t q f) -> c t q r g f", g=GROUPS, r=QUAD, q=QUADRANTS, t=TILES)
    x_by_chunk = x.rearrange("(c q b j) d -> c q j b d", q=QUADRANTS, b=ROW_BLOCKS, j=QUAD)
    loops_by_block = self_loop.rearrange("(c q b j) -> b c q j", q=QUADRANTS, b=ROW_BLOCKS, j=QUAD)
    out_by_chunk = out.rearrange("(c q b j) d -> c q j b d", q=QUADRANTS, b=ROW_BLOCKS, j=QUAD)

    with ExitStack() as ctx:
        def sbuf(name, shape, dtype=f32):
            return ctx.enter_context(nc.sbuf_tensor(name, shape, dtype))

        def psum(name, shape):
            return ctx.enter_context(nc.psum_tensor(name, shape, f32))

        def sem(name):
            return ctx.enter_context(nc.semaphore(name))

        raw = sbuf("raw", [P, TILES, GROUPS, QUAD_COLUMNS])
        turned = sbuf("turned", [P, RING, 2, CHUNK])
        high = sbuf("high", [P, PART_RING, 2, CHUNK], f32r)
        low = sbuf("low", [P, PART_RING, 2, CHUNK], f32r)
        x_rows = sbuf("x_rows", [P, BLOCKS, FEATURES])
        x_blocks = sbuf("x_blocks", [P, BLOCKS, FEATURES])
        x_high = sbuf("x_high", [P, SPLITS, 2, FEATURES], f32r)
        x_low = sbuf("x_low", [P, SPLITS, 2, FEATURES], f32r)
        x_chunk = sbuf("x_chunk", [P, ROW_BLOCKS, FEATURES])
        x_chunk_t = sbuf("x_chunk_t", [P, CHUNK])
        agg_t = sbuf("agg_t", [P, CHUNK])
        loops = x_chunk_t[:, :].rearrange("p (b c) -> p b c", b=ROW_BLOCKS)
        scale_diag, shift_diag, w2_scaled = [agg_t[:, FEATURES * i:FEATURES * (i + 1)] for i in range(3)]
        all_agg_t = sbuf("all_agg_t", [P, CHUNKS, CHUNK])
        halves = [all_agg_t[:, 2 * i:2 * i + 2, :].rearrange("p a (b c) -> p (a b) c", b=8) for i in range(3)]
        quarters = [all_agg_t[:, 6 + i, :].rearrange("p (a c) -> p a c", a=GROUPS) for i in range(2)]
        new = sbuf("new", [P, ROW_BLOCKS, FEATURES])
        w1 = new[:, 0:2, :].rearrange("p a d -> p (a d)")
        loops_raw = new[0:BLOCKS, 2, :]
        summed = [new, x_chunk, x_chunk_t[:, :].rearrange("p (b d) -> p b d", b=ROW_BLOCKS)]
        stats = sbuf("stats", [P, 2, ROW_BLOCKS, 6])
        mean_var = sbuf("mean_var", [P, 2, ROW_BLOCKS, 2])
        var_eps = sbuf("var_eps", [P, 2, ROW_BLOCKS])
        std = sbuf("std", [P, 2, ROW_BLOCKS])
        rstd = sbuf("rstd", [P, 2, ROW_BLOCKS])
        newton = sbuf("newton", [P, 2, ROW_BLOCKS])
        minus_mean = sbuf("minus_mean", [P, 2, ROW_BLOCKS])
        row_parts = sbuf("row_parts", [P, GROUPS, TILES])
        row_sums = sbuf("row_sums", [P, GROUPS])
        row_degrees = sbuf("row_degrees", [P, ROW_BLOCKS])
        degree = sbuf("degree", [P, ROW_BLOCKS])
        inv_looped = sbuf("inv_looped", [P, ROW_BLOCKS])
        inv_degree = sbuf("inv_degree", [P, BLOCKS])
        bn_stats = sbuf("bn_stats", [P, CHUNKS, 6])
        bn_mean_var = sbuf("bn_mean_var", [P, 2])
        bn_var_eps = sbuf("bn_var_eps", [P, 1])
        bn_std = sbuf("bn_std", [P, 1])
        bn_rstd = sbuf("bn_rstd", [P, 1])
        bn_newton = sbuf("bn_newton", [P, 1])
        bn_scale = sbuf("bn_scale", [P, 1])
        bn_mean = sbuf("bn_mean", [P, 1])
        bn_shift = sbuf("bn_shift", [P, 1])
        ident = sbuf("ident", [P, P])
        ones = sbuf("ones", [P, P])
        fold = sbuf("fold", [P, QUADRANTS, QUAD])
        loop_rows = sbuf("loop_rows", [P, BLOCKS])
        w0 = sbuf("w0", [P, FEATURES])
        w1_t = sbuf("w1_t", [P, 2, FEATURES])
        w2 = sbuf("w2", [P, FEATURES])
        w3_self = sbuf("w3_self", [P, FEATURES])
        w3_neighbour = sbuf("w3_neighbour", [P, FEATURES])
        bias0 = sbuf("bias0", [P, 1, FEATURES])
        bias1 = sbuf("bias1", [P, 1, FEATURES])
        bias2 = sbuf("bias2", [P, 1])
        gamma2 = sbuf("gamma2", [P, 1])
        beta2 = sbuf("beta2", [P, 1])
        agg = psum("agg", [P, 2, CHUNK])
        y = psum("y", [P, CHUNK])
        y_self = psum("y_self", [P, CHUNK])
        x_turned = psum("x_turned", [P, CHUNK])
        sums = psum("sums", [P, CHUNK])
        h = psum("h", [P, 2, CHUNK])
        y_rows = y[:, :].rearrange("p (b d) -> p b d", b=ROW_BLOCKS)
        h_rows = h[:, :, :].rearrange("p a (b d) -> p a b d", b=ROW_BLOCKS)
        y_self_rows = y_self[:, :].rearrange("p (b d) -> p b d", b=ROW_BLOCKS)

        def half_of(t):
            return halves[QUARTERED.index(t) % 2 if t in QUARTERED else 2]

        def quarter_of(t):
            return quarters[QUARTERED.index(t) % 2]

        def low_count(k, n):
            pairs = GPSIMD_LOW if n in GPSIMD_LOW else list(VECTOR_LOW)
            return len(pairs) * (k - CHUNKS) + pairs.index(n) + 1

        tile_loaded = [sem(f"tile_loaded_{t}") for t in range(TILES)]
        blocks_copied = sem("blocks_copied")
        rows_loaded = [sem(f"rows_loaded_{c}") for c in range(CHUNKS)]
        loops_loaded, loops_placed = sem("loops_loaded"), sem("loops_placed")
        constants_loaded, ones_made = sem("constants_loaded"), sem("ones_made")
        self_made = sem("self_made")
        bits_made, identity_made = sem("bits_made"), sem("identity_made")
        w1_turned, w1_copied = sem("w1_turned"), sem("w1_copied")
        pair_turned, pair_used = sem("pair_turned"), sem("pair_used")
        high_ready, low_ready = sem("high_ready"), sem("low_ready")
        vector_low_ready = sem("vector_low_ready")
        agg_copied, y_done, y_read = sem("agg_copied"), sem("y_done"), sem("y_read")
        chunk_staged, loops_made, loops_added = sem("chunk_staged"), sem("loops_made"), sem("loops_added")
        chunk_turned, chunk_t_copied = sem("chunk_turned"), sem("chunk_t_copied")
        half_folded, quarter_folded = sem("half_folded"), sem("quarter_folded")
        tile_summed, rows_summed = sem("tile_summed"), sem("rows_summed")
        degree_done, degree_copied = sem("degree_done"), sem("degree_copied")
        var_ready, std_ready, norm_ready = sem("var_ready"), sem("std_ready"), sem("norm_ready")
        x_normed, y_scaled, inv_ready = sem("x_normed"), sem("y_scaled"), sem("inv_ready")
        operand_high, operand_low = sem("operand_high"), sem("operand_low")
        bn_counted = sem("bn_counted")
        bn_var_ready, bn_std_ready = sem("bn_var_ready"), sem("bn_std_ready")
        scale_ready, shift_ready, scale_spread = sem("scale_ready"), sem("shift_ready"), sem("scale_spread")
        weights_scaled, h_done, h_copied = sem("weights_scaled"), sem("h_done"), sem("h_copied")
        leaky_done, residual_added = sem("leaky_done"), sem("residual_added")
        vector_step, stored = sem("vector_step"), sem("stored")
        block = ctx.enter_context(nc.Block())

        @block.sync
        def _(sp):
            def load(layer, c, t):
                k = CHUNKS * layer + c
                if not (is_number(k) and k == 0):
                    if layer == DEGREE or is_number(c) and c == 0 and layer == CONCAT:
                        sp.wait_ge(tile_summed, TILES * (k - 1) + t + 1)
                    else:
                        sp.wait_ge(pair_turned, PAIRS * (k - 1) + TILE_PAIRS * (t + 1))
                for q in (0, 2, 1, 3):
                    lanes = slice(QUAD * q, QUAD * (q + 1))
                    if is_number(c):
                        source = adj_tiles[c, t, q]
                    else:
                        source = adj_tiles[ds(c, 1), t, q].rearrange("a r g f -> (a r) g f")
                    sp.dma_start(raw[lanes, t, :, :], source).then_inc(tile_loaded[t], 16)

            def store(c):
                sp.wait_ge(x_normed, CHUNKS * SAGE + c + 1)
                for q in range(QUADRANTS):
                    if is_number(c):
                        target = out_by_chunk[c, q]
                    else:
                        target = out_by_chunk[ds(c, 1), q].rearrange("a j b d -> (a j) b d")
                    sp.dma_start(target, x_rows[QUAD * q:QUAD * (q + 1), ds(ROW_BLOCKS * c, ROW_BLOCKS), :],
                                 ).then_inc(stored, 16)

            for layer in range(LAYERS):
                for c in (0, 1):
                    for t in range(TILES):
                        load(layer, c, t)
                        if layer == DEGREE and c == 0:
                            for q in range(QUADRANTS):
                                sp.dma_start(x_rows[QUAD * q:QUAD * (q + 1), ROW_BLOCKS * t:ROW_BLOCKS * (t + 1), :],
                                             x_by_chunk[t, q]).then_inc(rows_loaded[t], 16)
                with sp.Fori(2, CHUNKS) as c:
                    for t in range(TILES):
                        load(layer, c, t)
                    if layer == SAGE:
                        store(c - 2)
            store(CHUNKS - 2)
            store(CHUNKS - 1)
            sp.wait_ge(stored, 16 * QUADRANTS * CHUNKS)

        @block.gpsimd
        def _(pool):
            nc.gpsimd.memset(ident[:, :], 0.0).then_inc(bits_made, 1)
            nc.gpsimd.memset(fold[:, :, :], 0.0).then_inc(bits_made, 1)
            pool.wait_ge(bits_made, 2)
            nc.gpsimd.affine_select(out=ident[:, :], in_=ident[:, :], compare_op=ALU.not_equal, fill=1.0,
                                    base=0, pattern=[[-1, P]], channel_multiplier=1).then_inc(identity_made, 1)
            pool.wait_ge(identity_made, 1)
            nc.gpsimd.memset(ones[:, :], 1.0).then_inc(ones_made, 1)
            quadrants = ident[:, :].rearrange("p (q j) -> p q j", q=QUADRANTS)
            for q in range(QUADRANTS):
                nc.gpsimd.tensor_tensor(fold[:, :, :], fold[:, :, :],
                                        quadrants[:, q:q + 1, :].to_broadcast([P, QUADRANTS, QUAD]),
                                        ALU.add).then_inc(identity_made, 1)
                pool.wait_ge(identity_made, q + 2)

            def fold_half(c, t):
                pool.wait_ge(tile_loaded[t], LOAD * (c + 1))
                if t in QUARTERED:
                    i = QUARTERED.index(t)
                    if not (is_number(c) and c == 0 and i < 2):
                        pool.wait_ge(quarter_folded, QUARTERS * c + i - 1)
                elif not (is_number(c) and c == 0 and t < TILES // 2):
                    pool.wait_ge(tile_summed, TILES * c + t - TILES // 2 + 1)
                nc.gpsimd.tensor_tensor(half_of(t), raw[:, t, :, 0:QUAD_COLUMNS // 2],
                                        raw[:, t, :, QUAD_COLUMNS // 2:QUAD_COLUMNS],
                                        ALU.add).then_inc(half_folded, 1)

            def fold_quarter(c, t):
                i = QUARTERED.index(t)
                pool.wait_ge(half_folded, TILES * c + t + 1)
                if i >= 2:
                    pool.wait_ge(tile_summed, TILES * c + QUARTERED[i - 2] + 1)
                elif not (is_number(c) and c == 0):
                    pool.wait_ge(tile_summed, TILES * (c - 1) + QUARTERED[i - 2] + 1)
                nc.gpsimd.tensor_tensor(quarter_of(t), half_of(t)[:, :, 0:QUAD_COLUMNS // 4],
                                        half_of(t)[:, :, QUAD_COLUMNS // 4:QUAD_COLUMNS // 2],
                                        ALU.add).then_inc(quarter_folded, 1)

            def fold_tile(c, t):
                fold_half(c, t)
                if t - 1 in QUARTERED:
                    fold_quarter(c, t - 1)

            def low_part(layer, c, n):
                s = SPLIT.index(n)
                pool.wait_ge(high_ready, SPLITS * (CHUNKS * (layer - 1) + c) + s + 1)
                nc.gpsimd.tensor_tensor(low[:, s % PART_RING], turned[:, slot_of(layer, n)],
                                        high[:, s % PART_RING].bitcast(f32),
                                        ALU.subtract).then_inc(low_ready, 1)

            def low_operand(layer, n):
                s = SPLIT.index(n)
                pool.wait_ge(operand_high, PAIRS * (layer - 1) + n + 1)
                nc.gpsimd.tensor_tensor(x_low[:, s], x_rows[:, 2 * n:2 * n + 2, :], x_high[:, s].bitcast(f32),
                                        ALU.subtract).then_inc(operand_low, 1)

            def add_residual(m):
                pool.wait_ge(leaky_done, m + 1)
                rows = summed[m % 3][:, :, :]
                nc.gpsimd.tensor_tensor(rows, rows, x_rows[:, ROW_BLOCKS * m:ROW_BLOCKS * (m + 1), :],
                                        ALU.add).then_inc(residual_added, 1)

            def low_operands(layer, *chunks):
                for n in SPLIT:
                    if n // TILE_PAIRS in chunks:
                        low_operand(layer, n)

            for t in range(TILES):
                fold_tile(0, t)
            with pool.Fori(1, CHUNKS - 1) as c:
                for t in range(TILES):
                    fold_tile(c, t)
            for t in range(TILES):
                fold_tile(CHUNKS - 1, t)
                if t >= 5:
                    low_operands(CONCAT, *FIRST_OPERANDS[t - 5])
            pool.wait_ge(constants_loaded, CONSTANTS)
            nc.gpsimd.tensor_tensor(w3_self[:, :], w3_self[:, :], ident[:, :], ALU.add).then_inc(self_made, 1)
            for layer in range(1, LAYERS):
                if layer - 1 != BATCHNORM:
                    for n in GPSIMD_LOW:
                        low_part(layer, 0, n)
                        if n == 13:
                            low_operands(layer, CHUNKS - 1)
                else:
                    for n in HIGH_BEFORE:
                        if n in GPSIMD_LOW:
                            low_part(layer, 0, n)
                    add_residual(0)
                    add_residual(1)
                    for m in range(CHUNKS):
                        if m + 2 < CHUNKS:
                            add_residual(m + 2)
                        low_operands(layer, m)
                        for n in HIGH_AFTER[m]:
                            if n in GPSIMD_LOW:
                                low_part(layer, 0, n)
                with pool.Fori(1, CHUNKS - 1) as c:
                    for n in GPSIMD_LOW:
                        low_part(layer, c, n)
                for n in GPSIMD_LOW:
                    low_part(layer, CHUNKS - 1, n)
                    if layer < BATCHNORM and n in OPERANDS_AFTER:
                        low_operands(layer + 1, *OPERANDS_AFTER[n])
                if layer < BATCHNORM:
                    low_operands(layer + 1, CHUNKS - 2)

        @block.scalar
        def _(act):
            def lanes(q):
                return slice(QUAD * q, QUAD * (q + 1))

            act.wait_ge(tile_loaded[1], LOAD)
            for b in range(ROW_BLOCKS):
                act.dma_start(new[CHUNKS * b:CHUNKS * (b + 1), 2, :].rearrange("c (q j) -> c q j", q=QUADRANTS),
                              loops_by_block[b]).then_inc(loops_loaded, 16)
            act.dma_start(w1, w_concat).then_inc(loops_loaded, 16)

            def load_constants():
                loads = [(w0[:, :], w_degree), (w2[:, :], w_batch), (w3_self[:, :], w_self),
                         (w3_neighbour[:, :], w_neighbour),
                         (bias0[:, 0, :], bias_degree.partition_broadcast(P)),
                         (bias1[:, 0, :], bias_concat.partition_broadcast(P))]
                loads += [(to[:, :], a.rearrange("(p a) -> p a", a=1))
                          for to, a in ((bias2, bias_batch), (gamma2, gamma), (beta2, shift_batch))]
                assert CONSTANTS == 16 * len(loads)
                for to, a in loads:
                    act.dma_start(to, a).then_inc(constants_loaded, 16)

            def high_part(layer, c, n):
                s = SPLIT.index(n)
                k = CHUNKS * layer + c
                act.wait_ge(pair_turned, PAIRS * k + n + 1)
                if s >= PART_RING:
                    act.wait_ge(pair_used, PAIRS * k + SPLIT[s - PART_RING] + 1)
                elif not (is_number(k) and k == CHUNKS):
                    act.wait_ge(pair_used, PAIRS * (k - 1) + SPLIT[s - PART_RING] + 1)
                nc.scalar.activation(high[:, s % PART_RING], turned[:, slot_of(layer, n)],
                                     ACT.Copy).then_inc(high_ready, 1)

            def copy_agg(layer, c, parity):
                e = CHUNKS * layer + c
                act.wait_ge(pair_used, PAIRS * (e + 1))
                by_block = agg[:, ds(parity, 1), :].rearrange("p a (q b j) -> p (a b) q j", q=QUADRANTS, b=ROW_BLOCKS)
                if layer == BATCHNORM:
                    to = all_agg_t[:, ds(c, 1), :].rearrange("p a (b q j) -> p (a b) q j", q=QUADRANTS, b=ROW_BLOCKS)
                else:
                    to = agg_t[:, :].rearrange("p (b q j) -> p b q j", q=QUADRANTS, b=ROW_BLOCKS)
                nc.scalar.activation(to, by_block, ACT.Copy).then_inc(agg_copied, 1)

            def stage_chunk(layer, c):
                e = CHUNKS * layer + c
                if layer == DEGREE:
                    if is_number(c) and c == 0:
                        act.wait_ge(identity_made, 1)
                    else:
                        act.wait_ge(loops_added, c)
                else:
                    before = 0 if layer == CONCAT else CHUNKS
                    if is_number(c) and c == 0 and layer == CONCAT:
                        act.wait_ge(loops_added, CHUNKS)
                    else:
                        act.wait_ge(chunk_turned, before + c)
                    act.wait_ge(x_normed, e - CHUNKS + 1)
                nc.scalar.activation(x_chunk[:, :, :], x_rows[:, ds(ROW_BLOCKS * c, ROW_BLOCKS), :],
                                     ACT.Copy).then_inc(chunk_staged, 1)
                if layer == DEGREE:
                    for b in range(ROW_BLOCKS):
                        made = nc.scalar.activation(loops[:, b, :], ident[:, :], ACT.Copy,
                                                    scale=loop_rows[:, ds(ROW_BLOCKS * c + b, 1)])
                    made.then_inc(loops_made, 1)

            def copy_chunk_t(layer, c):
                n = (0 if layer == CONCAT else CHUNKS) + c
                act.wait_ge(chunk_turned, n + 1)
                act.wait_ge(y_done, CHUNKS * layer + c)
                nc.scalar.activation(x_chunk_t[:, :], x_turned[:, :], ACT.Copy).then_inc(chunk_t_copied, 1)

            def copy_degrees(c):
                act.wait_ge(degree_done, c + 1)
                for q in range(QUADRANTS):
                    done = nc.scalar.activation(row_degrees[lanes(q), :],
                                                sums[lanes(q), ROW_BLOCKS * q:ROW_BLOCKS * (q + 1)], ACT.Copy)
                done.then_inc(degree_copied, 1)

            def by_degree(layer, c):
                inverse = inv_looped if layer == DEGREE else inv_degree
                if layer == DEGREE:
                    act.wait_ge(inv_ready, c + 1)
                act.wait_ge(y_done, CHUNKS * layer + c + 1)
                for b in range(ROW_BLOCKS):
                    at = b if layer == DEGREE else ds(ROW_BLOCKS * c + b, 1)
                    scale = inverse[:, b:b + 1] if layer == DEGREE else inverse[:, at]
                    done = nc.scalar.activation(new[:, b, :], y_rows[:, b, :], ACT.Copy, scale=scale)
                done.then_inc(y_scaled, 1)

            def root(layer, c, parity=0):
                act.wait_ge(var_ready, CHUNKS * layer + c + 1)
                nc.scalar.activation(std[:, parity, :], var_eps[:, parity, :], ACT.Sqrt).then_inc(std_ready, 1)

            def normalize(layer, c, rows, parity=0):
                act.wait_ge(norm_ready, CHUNKS * layer + c + 1)
                for b in range(ROW_BLOCKS):
                    to = x_rows[:, ds(ROW_BLOCKS * c + b, 1), :].rearrange("p a d -> p (a d)")
                    done = nc.scalar.activation(to, rows[:, b, :], ACT.Identity, scale=rstd[:, parity, b:b + 1],
                                                bias=minus_mean[:, parity, b:b + 1])
                done.then_inc(x_normed, 1)

            def high_operands(layer, *chunks):
                for m in chunks:
                    act.wait_ge(x_normed, CHUNKS * (layer - 1) + m + 1)
                    act.wait_ge(pair_used, PAIRS * (CHUNKS * layer - 1) + TILE_PAIRS * (m + 1))
                    for n in range(TILE_PAIRS * m, TILE_PAIRS * (m + 1)):
                        to = x_high[:, SPLIT.index(n)] if n in SPLIT else x_blocks[:, 2 * n:2 * n + 2, :]
                        nc.scalar.activation(to, x_rows[:, 2 * n:2 * n + 2, :], ACT.Copy).then_inc(operand_high, 1)

            for m in range(CHUNKS):
                if m == 4:
                    act.wait_ge(loops_placed, 1)
                    nc.scalar.activation(loop_rows[:, :].rearrange("p (c b) -> p b c", b=ROW_BLOCKS),
                                         sums[:, 0:BLOCKS].rearrange("p (b c) -> p b c", b=ROW_BLOCKS),
                                         ACT.Copy).then_inc(loops_placed, 1)
                    act.wait_ge(loops_placed, 2)
                    stage_chunk(DEGREE, 0)
                act.wait_ge(rows_loaded[m], LOAD)
                rows = slice(ROW_BLOCKS * m, ROW_BLOCKS * (m + 1))
                nc.scalar.activation(x_blocks[:, rows, :], x_rows[:, rows, :], ACT.Copy).then_inc(blocks_copied, 1)
            load_constants()
            act.wait_ge(w1_turned, 1)
            nc.scalar.activation(w1_t[:, :, :], x_turned[:, 0:2 * FEATURES].rearrange("p (a b) -> p a b", a=2),
                                 ACT.Copy).then_inc(w1_copied, 1)
            act.wait_ge(constants_loaded, CONSTANTS)
            with act.Fori(1, CHUNKS - 1) as c:
                copy_agg(DEGREE, c - 1, (c + 1) % 2)
                stage_chunk(DEGREE, c)
                copy_degrees(c - 1)
                by_degree(DEGREE, c - 1)
                root(DEGREE, c - 1)
                normalize(DEGREE, c - 1, new)
            copy_agg(DEGREE, CHUNKS - 2, 0)
            stage_chunk(DEGREE, CHUNKS - 1)
            copy_degrees(CHUNKS - 2)
            by_degree(DEGREE, CHUNKS - 2)
            high_operands(CONCAT, *FIRST_OPERANDS[0])
            root(DEGREE, CHUNKS - 2)
            high_operands(CONCAT, *FIRST_OPERANDS[1])
            normalize(DEGREE, CHUNKS - 2, new)
            high_operands(CONCAT, *FIRST_OPERANDS[2])

            def chunk(layer, c, before):
                first = is_number(c) and c == 0
                last = is_number(c) and not first and layer < BATCHNORM
                last_c = CHUNKS - 1 if first else c - 1
                root_at, norm_at = (11, 13) if before == DEGREE else (9, 11)
                for n in SPLIT:
                    high_part(layer, c, n)
                    if n == 2:
                        copy_agg(before, last_c, 1 if first else (c + 1) % 2)
                        if layer in (CONCAT, SAGE):
                            stage_chunk(layer, c)
                    if n == 6 and before == DEGREE:
                        copy_degrees(last_c)
                    if n == 6 and before in (DEGREE, SAGE):
                        by_degree(before, last_c)
                    if n == root_at and before != BATCHNORM:
                        root(before, last_c)
                    if n == norm_at and before != BATCHNORM:
                        normalize(before, last_c, new)
                    if n == norm_at and first:
                        high_operands(layer, CHUNKS - 1)
                    if last and n in OPERANDS_AFTER:
                        high_operands(layer + 1, *OPERANDS_AFTER[n])
                if layer in (CONCAT, SAGE):
                    copy_chunk_t(layer, c)
                if last:
                    high_operands(layer + 1, CHUNKS - 2)

            for layer in (CONCAT, BATCHNORM):
                chunk(layer, 0, layer - 1)
                with act.Fori(1, CHUNKS - 1) as c:
                    chunk(layer, c, layer)
                chunk(layer, CHUNKS - 1, layer)

            high_part(SAGE, 0, HIGH_BEFORE[0])
            copy_agg(BATCHNORM, CHUNKS - 1, 1)
            for n in HIGH_BEFORE[1:]:
                high_part(SAGE, 0, n)
            act.wait_ge(bn_var_ready, 1)
            nc.scalar.activation(bn_std[:, :], bn_var_eps[:, :], ACT.Sqrt).then_inc(bn_std_ready, 1)

            def copy_h(m):
                act.wait_ge(h_done, m + 1)
                nc.scalar.activation(summed[m % 3][:, :, :], h_rows[:, m % 2], ACT.Copy).then_inc(h_copied, 1)

            for m in range(3):
                copy_h(m)
            root(BATCHNORM, 0)
            for m in range(CHUNKS):
                normalize(BATCHNORM, m, summed[m % 3], m % 2)
                if m + 1 < CHUNKS:
                    root(BATCHNORM, m + 1, (m + 1) % 2)
                high_operands(SAGE, m)
                if m + 3 < CHUNKS:
                    copy_h(m + 3)
                for n in HIGH_AFTER[m]:
                    high_part(SAGE, 0, n)
            stage_chunk(SAGE, 0)
            copy_chunk_t(SAGE, 0)
            with act.Fori(1, CHUNKS) as c:
                chunk(SAGE, c, SAGE)
            copy_agg(SAGE, CHUNKS - 1, 1)
            by_degree(SAGE, CHUNKS - 1)
            root(SAGE, CHUNKS - 1)
            normalize(SAGE, CHUNKS - 1, new)

        @block.vector
        def _(dve):
            def turn(layer, c, n):
                k = CHUNKS * layer + c
                t, at = n // TILE_PAIRS, 2 * QUAD * (n % TILE_PAIRS)
                if n % TILE_PAIRS == 0:
                    dve.wait_ge(tile_loaded[t], LOAD * (k + 1))
                i = (SPLIT if n in SPLIT else NATIVE).index(n)
                first_ring = layer > DEGREE and is_number(k) and k == CHUNKS and i < (
                    SPLIT_RING if n in SPLIT else NATIVE_RING)
                if layer == DEGREE:
                    if not (is_number(k) and k == 0 and n < FIRST_RING):
                        dve.wait_ge(pair_used, PAIRS * k + n - FIRST_RING + 1)
                elif first_ring:
                    if slot_of(layer, n) < FIRST_RING:
                        dve.wait_ge(pair_used, PAIRS * k + slot_of(layer, n) - FIRST_RING + 1)
                elif n in NATIVE:
                    dve.wait_ge(pair_used, PAIRS * (k - (i < NATIVE_RING)) + NATIVE[i - NATIVE_RING] + 1)
                else:
                    held = SPLIT[i - SPLIT_RING]
                    dve.wait_ge(low_ready if held in GPSIMD_LOW else vector_low_ready,
                                low_count(k - (i < SPLIT_RING), held))
                nc.vector.transpose(turned[:, slot_of(layer, n)].rearrange("p b (g r) -> p g b r", g=GROUPS),
                                    raw[:, t, :, at:at + 2 * QUAD].rearrange("p g (b j) -> p g b j", b=2),
                                    ).then_inc(pair_turned, 1)

            def low_part(layer, c, n):
                s = SPLIT.index(n)
                dve.wait_ge(high_ready, SPLITS * (CHUNKS * (layer - 1) + c) + s + 1)
                nc.vector.tensor_tensor(low[:, s % PART_RING], turned[:, slot_of(layer, n)],
                                        high[:, s % PART_RING].bitcast(f32),
                                        ALU.subtract).then_inc(vector_low_ready, 1)

            def sum_tile(c, t):
                dve.wait_ge(pair_turned, PAIRS * c + TILE_PAIRS * (t + 1))
                if t in QUARTERED:
                    dve.wait_ge(quarter_folded, QUARTERS * c + QUARTERED.index(t) + 1)
                else:
                    dve.wait_ge(half_folded, TILES * c + t + 1)
                if t == 0 and not is_number(c):
                    dve.wait_ge(rows_summed, c)
                nc.vector.tensor_reduce(row_parts[:, :, t], quarter_of(t) if t in QUARTERED else half_of(t),
                                        AXIS.X, ALU.add).then_inc(tile_summed, 1)

            def sum_rows(c):
                dve.wait_ge(tile_summed, TILES * (c + 1))
                if not is_number(c):
                    dve.wait_ge(degree_done, c)
                nc.vector.tensor_reduce(row_sums[:, :], row_parts[:, :, :], AXIS.X, ALU.add).then_inc(rows_summed, 1)

            statistics_steps, refine_steps = 2, 4
            norm_steps = statistics_steps + refine_steps
            steps_of = [3 + 1 + norm_steps, 1 + norm_steps, norm_steps, norm_steps]
            first_step = [0]
            for layer in range(SAGE):
                first_step.append(first_step[-1] + CHUNKS * steps_of[layer] + (layer == BATCHNORM) * (refine_steps + 5))

            def stepper(base):
                done = [0]

                def step(instruction):
                    done[0] += 1
                    instruction.then_inc(vector_step, 1)
                    dve.wait_ge(vector_step, base + done[0])
                return step, done

            def row_statistics(rows, step, parity=0):
                for b in range(ROW_BLOCKS):
                    last = nc.vector.bn_stats(stats[:, parity, b, :], rows[:, b, :])
                step(last)

            def row_variances(step, parity=0):
                nc.vector.memset(var_eps[:, parity, :], EPS)
                for b in range(ROW_BLOCKS):
                    last = nc.vector.bn_aggr(mean_var[:, parity, b, :], stats[:, parity, b, :])
                step(last)
                nc.vector.tensor_tensor(var_eps[:, parity, :], mean_var[:, parity, :, 1], var_eps[:, parity, :],
                                        ALU.add).then_inc(var_ready, 1)

            def refine(step, r, root_of, square, scratch):
                step(nc.vector.reciprocal(r, root_of))
                step(nc.vector.scalar_tensor_tensor(out=scratch, in0=r, scalar=-0.5, in1=square,
                                                    op0=ALU.mult, op1=ALU.mult))
                step(nc.vector.tensor_tensor(scratch, scratch, r, ALU.mult))
                step(nc.vector.scalar_tensor_tensor(out=r, in0=scratch, scalar=1.5, in1=r,
                                                    op0=ALU.add, op1=ALU.mult))

            def norm_factors(e, step, parity=0):
                dve.wait_ge(std_ready, e + 1)
                refine(step, rstd[:, parity, :], std[:, parity, :], var_eps[:, parity, :], newton[:, parity, :])
                nc.vector.scalar_tensor_tensor(out=minus_mean[:, parity, :], in0=mean_var[:, parity, :, 0],
                                               scalar=-1.0, in1=rstd[:, parity, :], op0=ALU.mult,
                                               op1=ALU.mult).then_inc(norm_ready, 1)

            def epilogue(layer, c):
                e = CHUNKS * layer + c
                step, done = stepper(first_step[layer] + steps_of[layer] * c)
                rows = x_rows[:, ds(ROW_BLOCKS * c, ROW_BLOCKS), :]

                def invert():
                    blocks = ds(ROW_BLOCKS * c, ROW_BLOCKS)
                    dve.wait_ge(degree_copied, c + 1)
                    step(nc.vector.tensor_tensor(degree[:, :], row_degrees[:, :], loop_rows[:, blocks], ALU.add))
                    nc.vector.reciprocal(inv_looped[:, :], degree[:, :]).then_inc(inv_ready, 1)
                    dve.wait_ge(inv_ready, c + 1)
                    step(nc.vector.tensor_scalar(degree[:, :], row_degrees[:, :], 1.0, None, ALU.max))
                    step(nc.vector.reciprocal(inv_degree[:, blocks], degree[:, :]))

                def combine():
                    if layer == DEGREE:
                        dve.wait_ge(y_scaled, c + 1)
                        nc.vector.tensor_tensor(new[:, :, :], new[:, :, :],
                                                bias0[:, :, :].to_broadcast([P, ROW_BLOCKS, FEATURES]),
                                                ALU.add).then_inc(y_read, 1)
                        dve.wait_ge(y_read, e + 1)
                        step(nc.vector.tensor_tensor(new[:, :, :], new[:, :, :], rows, ALU.add))
                    elif layer == CONCAT:
                        dve.wait_ge(y_done, e + 1)
                        nc.vector.tensor_tensor(new[:, :, :], y_rows,
                                                bias1[:, :, :].to_broadcast([P, ROW_BLOCKS, FEATURES]),
                                                ALU.add).then_inc(y_read, 1)
                        dve.wait_ge(y_read, e + 1)
                        step(nc.vector.scalar_tensor_tensor(out=new[:, :, :], in0=new[:, :, :], scalar=0.0,
                                                            in1=rows, op0=ALU.max, op1=ALU.add))
                    elif layer == BATCHNORM:
                        dve.wait_ge(y_done, e + 1)
                        nc.vector.bn_stats(bn_stats[:, ds(c, 1), :].rearrange("p a n -> p (a n)"),
                                           y[:, :]).then_inc(y_read, 1)
                    else:
                        dve.wait_ge(y_scaled, CHUNKS + c + 1)
                        nc.vector.tensor_tensor(new[:, :, :], new[:, :, :], y_self_rows, ALU.add).then_inc(y_read, 1)

                def statistics():
                    if layer == SAGE:
                        dve.wait_ge(y_read, e + 1)
                    if layer != BATCHNORM:
                        row_statistics(new, step)

                def variances():
                    if layer != BATCHNORM:
                        row_variances(step)

                def factors():
                    if layer != BATCHNORM:
                        norm_factors(e, step)
                        assert done[0] == steps_of[layer], (layer, done[0])

                return (invert if layer == DEGREE else None), combine, statistics, variances, factors

            def chunk(layer, c, before, last_c):
                invert, *parts = epilogue(before, last_c) if before is not None else [None]
                at = (9, 10, 11, 12)
                for n in range(PAIRS):
                    turn(layer, c, n)
                    if before == DEGREE and n in (1, 3):
                        sum_tile(last_c, TILES - 2 + n // TILE_PAIRS)
                        if n == 3:
                            sum_rows(last_c)
                    if n == at[0] - 2 and invert:
                        invert()
                    if n in at and parts:
                        parts[at.index(n)]()
                    for pair, after in VECTOR_LOW.items():
                        if layer != DEGREE and n == after:
                            low_part(layer, c, pair)
                    if layer == DEGREE and n >= 5 and n % TILE_PAIRS == 1:
                        sum_tile(c, n // TILE_PAIRS - 2)

            chunk(DEGREE, 0, None, None)
            for c in range(CHUNKS):
                dve.wait_ge(rows_loaded[c], LOAD)
            dve.wait_ge(loops_placed, 2)
            with dve.Fori(1, CHUNKS) as c:
                chunk(DEGREE, c, DEGREE, c - 1)
            for layer in (CONCAT, BATCHNORM):
                chunk(layer, 0, layer - 1, CHUNKS - 1)
                with dve.Fori(1, CHUNKS) as c:
                    chunk(layer, c, layer, c - 1)

            for n in TURNED_BEFORE[0]:
                turn(SAGE, 0, n)
            _, combine, _, _, _ = epilogue(BATCHNORM, CHUNKS - 1)
            combine()
            step, done = stepper(first_step[BATCHNORM])
            dve.wait_ge(y_read, CHUNKS * SAGE)
            nc.vector.bn_aggr(bn_mean_var[:, :], bn_stats[:, :, :].rearrange("p c s -> p (c s)")).then_inc(bn_counted, 1)
            dve.wait_ge(bn_counted, 1)
            nc.vector.tensor_scalar(bn_var_eps[:, :], bn_mean_var[:, 1:2], EPS, None, ALU.add).then_inc(bn_var_ready, 1)
            step(nc.vector.tensor_tensor(bn_mean[:, :], bn_mean_var[:, 0:1], bias2[:, :], ALU.add))
            step(nc.vector.tensor_tensor(bn_mean[:, :], bias2[:, :], bn_mean[:, :], ALU.subtract))
            dve.wait_ge(bn_std_ready, 1)
            refine(step, bn_rstd[:, :], bn_std[:, :], bn_var_eps[:, :], bn_newton[:, :])
            step(nc.vector.tensor_tensor(bn_scale[:, :], gamma2[:, :], bn_rstd[:, :], ALU.mult))
            nc.vector.tensor_scalar(scale_diag, ident[:, :], bn_scale[:, 0:1], None, ALU.mult,
                                    ).then_inc(scale_ready, 1)
            step(nc.vector.tensor_tensor(bn_shift[:, :], bn_mean[:, :], bn_scale[:, :], ALU.mult))
            step(nc.vector.tensor_tensor(bn_shift[:, :], bn_shift[:, :], beta2[:, :], ALU.add))
            nc.vector.tensor_scalar(shift_diag, ident[:, :], bn_shift[:, 0:1], None, ALU.mult,
                                    ).then_inc(shift_ready, 1)
            dve.wait_ge(scale_spread, 1)
            nc.vector.tensor_tensor(w2_scaled, sums[:, 0:FEATURES], w2[:, :], ALU.mult).then_inc(weights_scaled, 1)

            def leaky(m):
                dve.wait_ge(h_copied, m + 1)
                rows = summed[m % 3][:, :, :]
                nc.vector.scalar_tensor_tensor(out=rows, in0=h_rows[:, m % 2], scalar=SLOPE, in1=rows,
                                               op0=ALU.mult, op1=ALU.max).then_inc(leaky_done, 1)

            def chunk_statistics(m):
                dve.wait_ge(residual_added, m + 1)
                row_statistics(summed[m % 3], step, m % 2)
                row_variances(step, m % 2)

            low_part(SAGE, 0, EARLY_LOW)
            for n in TURNED_BEFORE[1]:
                turn(SAGE, 0, n)
            leaky(0)
            leaky(1)
            chunk_statistics(0)
            for m in range(CHUNKS):
                norm_factors(CHUNKS * BATCHNORM + m, step, m % 2)
                if m + 2 < CHUNKS:
                    leaky(m + 2)
                if m + 1 < CHUNKS:
                    chunk_statistics(m + 1)
                if m == 5:
                    low_part(SAGE, 0, LATE_LOW)
                for n in TURNED_AFTER[m]:
                    turn(SAGE, 0, n)
            assert first_step[BATCHNORM] + done[0] == first_step[SAGE], done[0]
            with dve.Fori(1, CHUNKS) as c:
                chunk(SAGE, c, SAGE, c - 1)
            for part in epilogue(SAGE, CHUNKS - 1)[1:]:
                part()

        @block.tensor
        def _(pe):
            def multiply(layer, c, n):
                k = CHUNKS * layer + c
                first = is_number(c) and c == 0
                into = agg[:, 0, :] if first else agg[:, ds(c % 2, 1), :].rearrange("p a n -> p (a n)")
                if layer == DEGREE or n not in SPLIT:
                    operands = x_blocks
                    if first and layer == DEGREE:
                        operands = x_rows
                        if n % TILE_PAIRS == 0:
                            pe.wait_ge(rows_loaded[n // TILE_PAIRS], LOAD)
                    elif first and layer > DEGREE:
                        pe.wait_ge(operand_high, PAIRS * (layer - 1) + n + 1)
                    pe.wait_ge(pair_turned, PAIRS * k + n + 1)
                    for b in range(2):
                        last = nc.tensor.matmul(into, operands[:, 2 * n + b, :], turned[:, slot_of(layer, n), b, :],
                                                start=n == 0 and b == 0, stop=n == PAIRS - 1 and b == 1)
                else:
                    s = SPLIT.index(n)
                    if first:
                        pe.wait_ge(operand_low, SPLITS * (layer - 1) + s + 1)
                    pe.wait_ge(high_ready, SPLITS * (k - CHUNKS) + s + 1)
                    for b in range(2):
                        for part in (x_high[:, s], x_low[:, s]):
                            nc.tensor.matmul(into, part[:, b, :], high[:, s % PART_RING, b, :],
                                             start=False, stop=False)
                    pe.wait_ge(low_ready if n in GPSIMD_LOW else vector_low_ready, low_count(k, n))
                    for b in range(2):
                        last = nc.tensor.matmul(into, x_high[:, s, b, :], low[:, s % PART_RING, b, :],
                                                start=False, stop=n == PAIRS - 1 and b == 1)
                last.then_inc(pair_used, 1)

            def place_loops():
                pe.wait_ge(loops_loaded, LOOPS)
                pe.wait_ge(identity_made, 1)
                nc.tensor.transpose(sums[:, 0:BLOCKS], loops_raw,
                                    ident[0:BLOCKS, 0:BLOCKS]).then_inc(loops_placed, 1)

            def own_rows(layer, c):
                if layer == DEGREE:
                    into = agg[:, ds(c % 2, 1), :].rearrange("p a (q b j) -> p (a b) q j", q=QUADRANTS, b=ROW_BLOCKS)
                    if is_number(c) and c == 0:
                        pe.wait_ge(identity_made, 1 + QUADRANTS)
                        pe.wait_ge(ones_made, 1)
                        for a in range(2):
                            last = nc.tensor.transpose(x_turned[:, FEATURES * a:FEATURES * (a + 1)],
                                                       w1[:, FEATURES * a:FEATURES * (a + 1)], ident[:, :])
                        last.then_inc(w1_turned, 1)
                    pe.wait_ge(loops_made, c + 1)
                    for b in range(ROW_BLOCKS):
                        last = nc.tensor.matmul(into[:, b], x_chunk[:, b, :],
                                                loops[:, b, :].rearrange("p (q j) -> p q j", q=QUADRANTS),
                                                start=False, stop=False)
                    last.then_inc(loops_added, 1)
                elif layer != BATCHNORM:
                    pe.wait_ge(chunk_staged, CHUNKS * (1 if layer == CONCAT else 2) + c + 1)
                    before = (0 if layer == CONCAT else CHUNKS) + c
                    if not (is_number(before) and before == 0):
                        pe.wait_ge(chunk_t_copied, before)
                    else:
                        pe.wait_ge(w1_copied, 1)
                    for b in range(ROW_BLOCKS):
                        last = nc.tensor.transpose(x_turned[:, P * b:P * (b + 1)], x_chunk[:, b, :], ident[:, :])
                    last.then_inc(chunk_turned, 1)

            def weights(layer, c):
                e = CHUNKS * layer + c
                if layer == DEGREE:
                    pe.wait_ge(rows_summed, c + 1)
                    nc.tensor.matmul(sums[:, 0:GROUPS], fold[:, :, :].rearrange("p u j -> p (u j)"), row_sums[:, :],
                                     start=True, stop=True).then_inc(degree_done, 1)
                pe.wait_ge(agg_copied, e + 1)
                if is_number(e) and e > 0 and c == CHUNKS - 1 and layer == SAGE:
                    pe.wait_ge(y_read, e)
                if layer in (CONCAT, SAGE):
                    pe.wait_ge(chunk_t_copied, (0 if layer == CONCAT else CHUNKS) + c + 1)
                if layer == BATCHNORM:
                    last = nc.tensor.matmul(y[:, :], w2[:, :], all_agg_t[:, ds(c, 1), :].rearrange("p a n -> p (a n)"),
                                            start=True, stop=True)
                for b in range(ROW_BLOCKS if layer != BATCHNORM else 0):
                    cols = slice(P * b, P * (b + 1))
                    if layer == DEGREE:
                        last = nc.tensor.matmul(y[:, cols], agg_t[:, cols], w0[:, :], start=True, stop=True)
                    elif layer == CONCAT:
                        nc.tensor.matmul(y[:, cols], x_chunk_t[:, cols], w1_t[:, 0, :], start=True, stop=False)
                        last = nc.tensor.matmul(y[:, cols], agg_t[:, cols], w1_t[:, 1, :], start=False, stop=True)
                    else:
                        nc.tensor.matmul(y_self[:, cols], x_chunk_t[:, cols], w3_self[:, :], start=True, stop=True)
                        last = nc.tensor.matmul(y[:, cols], agg_t[:, cols], w3_neighbour[:, :], start=True, stop=True)
                last.then_inc(y_done, 1)

            def chunk(layer, c, before, last_c):
                for n in range(PAIRS):
                    multiply(layer, c, n)
                    if is_number(c) and c == 0 and layer == DEGREE and n == 7:
                        place_loops()
                    if before is not None and n == (3 if before == DEGREE else 1):
                        weights(before, last_c)
                    if n == 12:
                        own_rows(layer, c)

            def batch_normed(m):
                if m >= 2:
                    pe.wait_ge(leaky_done, m - 1)
                for b in range(ROW_BLOCKS):
                    cols = slice(P * b, P * (b + 1))
                    nc.tensor.matmul(h[:, m % 2, cols], ones[:, :], shift_diag, start=True, stop=False)
                    last = nc.tensor.matmul(h[:, m % 2, cols], all_agg_t[:, m, cols], w2_scaled,
                                            start=False, stop=True)
                last.then_inc(h_done, 1)

            for layer in (DEGREE, CONCAT, BATCHNORM):
                chunk(layer, 0, layer - 1 if layer else None, CHUNKS - 1)
                if layer == DEGREE:
                    pe.wait_ge(blocks_copied, CHUNKS)
                with pe.Fori(1, CHUNKS) as c:
                    chunk(layer, c, layer, c - 1)
            weights(BATCHNORM, CHUNKS - 1)
            pe.wait_ge(scale_ready, 1)
            nc.tensor.matmul(sums[:, 0:FEATURES], ones[:, :], scale_diag, start=True,
                             stop=True).then_inc(scale_spread, 1)
            pe.wait_ge(shift_ready, 1)
            pe.wait_ge(weights_scaled, 1)
            for m in range(5):
                batch_normed(m)
            for n in range(PAIRS):
                multiply(SAGE, 0, n)
                if n % TILE_PAIRS and n // TILE_PAIRS + 5 < CHUNKS:
                    batch_normed(n // TILE_PAIRS + 5)
                if n == 12:
                    own_rows(SAGE, 0)
            pe.wait_ge(self_made, 1)
            with pe.Fori(1, CHUNKS) as c:
                chunk(SAGE, c, SAGE, c - 1)
            weights(SAGE, CHUNKS - 1)


_INS = ["x", "adj", "L0_gnn_kernel", "L0_gnn_bias", "L0_gnn_beta", "L1_gnn_W", "L1_gnn_b", "L2_gnn_W", "L2_gnn_b",
        "L2_gnn_gamma", "L2_gnn_beta", "L3_gnn_W_self", "L3_gnn_W_neigh"]


def kernel(**inputs):
    import numpy as np
    import concourse.bacc as bacc
    from concourse.bass_utils import run_bass_kernel_spmd

    nc = bacc.Bacc("TRN2", target_bir_lowering=False, num_devices=1)
    arrays, args = {}, []
    for name in _INS:
        a = np.ascontiguousarray(inputs[name])
        arrays[f"in_{name}"] = a
        args.append(nc.dram_tensor(f"in_{name}", a.shape, mybir.dt.from_np(a.dtype), kind="ExternalInput").ap())
    args.append(nc.dram_tensor("out", (NODES, FEATURES), mybir.dt.float32, kind="ExternalOutput").ap())
    gnn_layers(nc, *args)
    return run_bass_kernel_spmd(nc, [arrays], core_ids=[0]).results[0]["out"]
```
